# Optimizing a Trainium2 kernel written in Bass

```python
import numpy as np
import jax
import jax.numpy as jnp

def _softmax(x, axis=-1):
    return jax.nn.softmax(x, axis=axis)

def _gelu(x):
    return jax.nn.gelu(x, approximate=True)

def _silu(x):
    return jax.nn.silu(x)

def _sigmoid(x):
    return jax.nn.sigmoid(x)

def _layernorm(x, axis=-1, eps=1e-05):
    m = jnp.mean(x, axis=axis, keepdims=True)
    v = jnp.var(x, axis=axis, keepdims=True)
    return (x - m) / jnp.sqrt(v + eps)

def _scatter_add(tgt, idx, src, axis=0):
    return tgt.at[idx].add(src)

def _segment_sum(src, seg, n):
    return jax.ops.segment_sum(src, seg, n)
kernel_name = 'mk_decoder_preln_d1_seqx_r4_e0352e'

def setup_inputs(seed: int=0):
    np.random.seed(seed)
    _w = jnp.asarray

    def _rec_inputs():
        import jax
        import jax.numpy as jnp
        _rk = jax.random.key(seed)
        x = -0.0002928 + 1 * jax.random.normal(jax.random.fold_in(_rk, 1), (4, 512, 256), jnp.float32)
        _lenS = 512 - jax.random.randint(jax.random.fold_in(_rk, 7), (4,), 0, max(1, 512 // 4) + 1, jnp.int32)
        _lenS2 = 1601 - jax.random.randint(jax.random.fold_in(_rk, 8), (4,), 0, max(1, 1601 // 4) + 1, jnp.int32)
        _ctx_1024P = jax.random.normal(jax.random.fold_in(_rk, 11), (4, 16, 256), jnp.float32)
        _ctx_1024c = jax.random.dirichlet(jax.random.fold_in(_rk, 511), 0.3 * jnp.ones((16,), jnp.float32), (4, 1601))
        _ctx_1024t = jnp.einsum('bsk,bkd->bsd', _ctx_1024c, _ctx_1024P)
        _ctx_1024t = _ctx_1024t * jax.lax.rsqrt(jnp.mean(jnp.square(_ctx_1024t)) + 1e-12) * 0.953939
        ctx_1024 = -1.39393e-06 + 0.999914 * (_ctx_1024t + 0.3 * jax.random.normal(jax.random.fold_in(_rk, 611), (4, 1601, 256), jnp.float32))
        return (x, ctx_1024)
    x, ctx_1024 = _rec_inputs()

    def _L0_attn_setup():
        import jax, jax.numpy as jnp
        import numpy as np
        N_HEADS = 16
        D_MODEL = 256
        D_HEAD = 64
        MAX_SEQ_LEN = 256

        def _pos_bias(rel_pos_bias, T):
            i = jnp.arange(T)[:, None]
            j = jnp.arange(T)[None, :]
            idx = jnp.clip(MAX_SEQ_LEN - 1 - (i - j), 0, MAX_SEQ_LEN - 1)
            bias = rel_pos_bias[:, idx]
            return jnp.where((j <= i)[None], bias, 0.0)
        key = jax.random.key(seed)
        ks = jax.random.split(key, 7)
        std = np.sqrt(2.0 / (D_MODEL + D_HEAD)).astype(np.float32)
        hd = N_HEADS * D_HEAD
        Wq = jax.random.normal(ks[0], (D_MODEL, hd), jnp.float32) * std
        Wk = jax.random.normal(ks[1], (D_MODEL, hd), jnp.float32) * std
        Wv = jax.random.normal(ks[2], (D_MODEL, hd), jnp.float32) * std
        Wo = jax.random.normal(ks[3], (hd, D_MODEL), jnp.float32) * (1.0 / np.sqrt(hd))
        bo = jnp.zeros((D_MODEL,), jnp.float32)
        rel_pos_bias = jax.random.normal(ks[4], (N_HEADS, MAX_SEQ_LEN), jnp.float32) * 0.02
        x = jax.random.normal(ks[5], (4, 256, D_MODEL), jnp.float32)
        return {'x': x, 'Wq': Wq, 'Wk': Wk, 'Wv': Wv, 'Wo': Wo, 'bo': bo, 'rel_pos_bias': rel_pos_bias}
    _L0_attn_all = _L0_attn_setup()
    _L0_attn_in = {k: v for k, v in _L0_attn_all.items() if k in ('Wq', 'Wk', 'Wv', 'Wo', 'bo', 'rel_pos_bias')}
    del _L0_attn_all

    def _L0_xattn_setup():
        import jax, jax.numpy as jnp
        import numpy as np
        DIM = 256
        H = 16
        DH = DIM // H
        EPS = 1.1920928955078125e-07

        def _rms_norm(t, gamma):
            var = jnp.mean(jnp.square(t), axis=-1, keepdims=True)
            return t * jax.lax.rsqrt(var + EPS) * gamma
        key = jax.random.key(seed)
        ks = jax.random.split(key, 6)
        b, n, m = (2, 512, 512)
        x = jax.random.normal(ks[0], (b, n, DIM), dtype=jnp.float32)
        c = jax.random.normal(ks[1], (b, m, DIM), dtype=jnp.float32)
        Wq = jax.random.normal(ks[2], (DIM, DIM), dtype=jnp.float32) * 0.02
        bq = jnp.zeros((DIM,), dtype=jnp.float32)
        Wkv = jax.random.normal(ks[3], (2 * DIM, DIM), dtype=jnp.float32) * 0.02
        bkv = jnp.zeros((2 * DIM,), dtype=jnp.float32)
        q_gamma = jnp.ones((DH,), dtype=jnp.float32)
        k_gamma = jnp.ones((DH,), dtype=jnp.float32)
        return {'x': x, 'c': c, 'Wq': Wq, 'bq': bq, 'Wkv': Wkv, 'bkv': bkv, 'q_gamma': q_gamma, 'k_gamma': k_gamma}
    _L0_xattn_all = _L0_xattn_setup()
    _L0_xattn_in = {k: v for k, v in _L0_xattn_all.items() if k in ('Wq', 'bq', 'Wkv', 'bkv', 'q_gamma', 'k_gamma')}
    del _L0_xattn_all

    def _L0_ffn_setup():
        import jax, jax.numpy as jnp
        import numpy as np
        B, S, H = (2, 512, 256)
        I = 128
        E_R, E_Z = (32, 8)
        E_T = E_R + E_Z
        K = 6
        SCALE = 2.5
        W_INIT = 0.02
        key = jax.random.key(seed)
        k0, k1, k2, k3 = jax.random.split(key, 4)
        return {'hidden_states': jax.random.normal(k0, (B, S, H), jnp.float32), 'classifier_weight': jax.random.normal(k1, (E_T, H), jnp.float32) * W_INIT, 'e_score_correction_bias': jnp.zeros((E_T,), jnp.float32), 'gate_up_proj': jax.random.normal(k2, (E_T, 2 * I, H), jnp.float32) * W_INIT, 'down_proj': jax.random.normal(k3, (E_R, H, I), jnp.float32) * W_INIT}
    _L0_ffn_all = _L0_ffn_setup()
    _L0_ffn_in = {k: v for k, v in _L0_ffn_all.items() if k in ('classifier_weight', 'e_score_correction_bias', 'gate_up_proj', 'down_proj')}
    del _L0_ffn_all
    return {'x': x, 'ctx_1024': ctx_1024, 'L0_attn_Wq': _L0_attn_in['Wq'], 'L0_attn_Wk': _L0_attn_in['Wk'], 'L0_attn_Wv': _L0_attn_in['Wv'], 'L0_attn_Wo': _L0_attn_in['Wo'], 'L0_attn_bo': _L0_attn_in['bo'], 'L0_attn_rel_pos_bias': _L0_attn_in['rel_pos_bias'], 'L0_xattn_Wq': _L0_xattn_in['Wq'], 'L0_xattn_bq': _L0_xattn_in['bq'], 'L0_xattn_Wkv': _L0_xattn_in['Wkv'], 'L0_xattn_bkv': _L0_xattn_in['bkv'], 'L0_xattn_q_gamma': _L0_xattn_in['q_gamma'], 'L0_xattn_k_gamma': _L0_xattn_in['k_gamma'], 'L0_ffn_classifier_weight': _L0_ffn_in['classifier_weight'], 'L0_ffn_e_score_correction_bias': _L0_ffn_in['e_score_correction_bias'], 'L0_ffn_gate_up_proj': _L0_ffn_in['gate_up_proj'], 'L0_ffn_down_proj': _L0_ffn_in['down_proj']}

def reference(x, ctx_1024, L0_attn_Wq, L0_attn_Wk, L0_attn_Wv, L0_attn_Wo, L0_attn_bo, L0_attn_rel_pos_bias, L0_xattn_Wq, L0_xattn_bq, L0_xattn_Wkv, L0_xattn_bkv, L0_xattn_q_gamma, L0_xattn_k_gamma, L0_ffn_classifier_weight, L0_ffn_e_score_correction_bias, L0_ffn_gate_up_proj, L0_ffn_down_proj):
    import jax
    import jax.numpy as jnp

    def _L0_attn_ref(x, Wq, Wk, Wv, Wo, bo, rel_pos_bias):
        import jax, jax.numpy as jnp
        import numpy as np
        N_HEADS = 16
        D_MODEL = 256
        D_HEAD = 64
        MAX_SEQ_LEN = 256

        def _pos_bias(rel_pos_bias, T):
            i = jnp.arange(T)[:, None]
            j = jnp.arange(T)[None, :]
            idx = jnp.clip(MAX_SEQ_LEN - 1 - (i - j), 0, MAX_SEQ_LEN - 1)
            bias = rel_pos_bias[:, idx]
            return jnp.where((j <= i)[None], bias, 0.0)
        B, T, _ = x.shape
        H, dh = (N_HEADS, D_HEAD)
        q = (x @ Wq).reshape(B, T, H, dh).transpose(0, 2, 1, 3)
        k = (x @ Wk).reshape(B, T, H, dh).transpose(0, 2, 1, 3)
        v = (x @ Wv).reshape(B, T, H, dh).transpose(0, 2, 1, 3)
        logits = jnp.einsum('bhqd,bhkd->bhqk', q, k)
        i = jnp.arange(T)[:, None]
        j = jnp.arange(T)[None, :]
        causal = jnp.where(j > i, -jnp.inf, 0.0)
        logits = logits + causal[None, None] + _pos_bias(rel_pos_bias, T)[None]
        logits = logits / dh
        probs = jax.nn.softmax(logits, axis=-1)
        out = jnp.einsum('bhqk,bhkd->bhqd', probs, v)
        out = out.transpose(0, 2, 1, 3).reshape(B, T, H * dh)
        return out @ Wo + bo

    def _L0_xattn_ref(x, c, Wq, bq, Wkv, bkv, q_gamma, k_gamma):
        import jax, jax.numpy as jnp
        import numpy as np
        DIM = 256
        H = 16
        DH = DIM // H
        EPS = 1.1920928955078125e-07

        def _rms_norm(t, gamma):
            var = jnp.mean(jnp.square(t), axis=-1, keepdims=True)
            return t * jax.lax.rsqrt(var + EPS) * gamma
        b, n, _ = x.shape
        m = c.shape[1]
        q = x @ Wq.T + bq
        q = q.reshape(b, n, H, DH).transpose(0, 2, 1, 3)
        kv = c @ Wkv.T + bkv
        kv = kv.reshape(b, m, H, DH, 2).transpose(0, 2, 1, 3, 4)
        k = kv[..., 0]
        v = kv[..., 1]
        q = _rms_norm(q, q_gamma)
        k = _rms_norm(k, k_gamma)
        scale = 1.0 / jnp.sqrt(jnp.asarray(DH, dtype=q.dtype))
        scores = jnp.einsum('bhnd,bhmd->bhnm', q, k) * scale
        attn = jax.nn.softmax(scores, axis=-1)
        out = jnp.einsum('bhnm,bhmd->bhnd', attn, v)
        out = out.transpose(0, 2, 1, 3).reshape(b, n, H * DH)
        return out

    def _L0_ffn_ref(hidden_states, classifier_weight, e_score_correction_bias, gate_up_proj, down_proj):
        import jax, jax.numpy as jnp
        import numpy as np
        B, S, H = (2, 512, 256)
        I = 128
        E_R, E_Z = (32, 8)
        E_T = E_R + E_Z
        K = 6
        SCALE = 2.5
        W_INIT = 0.02
        orig_shape = hidden_states.shape
        x = hidden_states.reshape(-1, H).astype(jnp.float32)
        T = x.shape[0]
        logits = x @ classifier_weight.T
        scores = jax.nn.softmax(logits, axis=-1)
        _, topk_idx = jax.lax.top_k(scores + e_score_correction_bias[None, :], K)
        topk_w = jnp.take_along_axis(scores, topk_idx, axis=1) * SCALE
        w_full = jnp.zeros((T, E_T), jnp.float32).at[jnp.arange(T)[:, None], topk_idx].add(topk_w)
        zero_w = w_full[:, E_R:].sum(axis=-1, keepdims=True)
        out0 = x * zero_w
        routed_w = w_full[:, :E_R].T

        def body(out, xs):
            Wgu, Wd, we = xs
            gate, up = jnp.split(x @ Wgu.T, 2, axis=-1)
            y = jax.nn.silu(gate) * up @ Wd.T
            return (out + we[:, None] * y, None)
        out, _ = jax.lax.scan(body, out0, (gate_up_proj[:E_R], down_proj, routed_w))
        return out.reshape(orig_shape).astype(hidden_states.dtype)
    x = x + _L0_attn_ref(_layernorm(x, axis=-1), L0_attn_Wq, L0_attn_Wk, L0_attn_Wv, L0_attn_Wo, L0_attn_bo, L0_attn_rel_pos_bias)
    x = x + _L0_xattn_ref(_layernorm(x, axis=-1), ctx_1024, L0_xattn_Wq, L0_xattn_bq, L0_xattn_Wkv, L0_xattn_bkv, L0_xattn_q_gamma, L0_xattn_k_gamma)
    x = x + _L0_ffn_ref(_layernorm(x, axis=-1), L0_ffn_classifier_weight, L0_ffn_e_score_correction_bias, L0_ffn_gate_up_proj, L0_ffn_down_proj)
    return x

_drawn_inputs = setup_inputs


def setup_inputs(seed=0):
    import zlib

    import numpy as np

    out = dict(_drawn_inputs(seed))
    spreads = {'L0_attn_bo': (0.0, 0.1),
     'L0_xattn_bq': (0.0, 0.488),
     'L0_xattn_bkv': (0.0, 0.1),
     'L0_xattn_q_gamma': (1.0, 0.6),
     'L0_xattn_k_gamma': (1.0, 0.6),
     'L0_ffn_e_score_correction_bias': (0.0, 0.1)}
    factors = {'L0_attn_rel_pos_bias': 200.0, 'L0_ffn_gate_up_proj': 8.0, 'L0_ffn_down_proj': 8.0}
    for name, (base, spread) in spreads.items():
        noise = np.random.default_rng([zlib.crc32(name.encode()), seed]).standard_normal(out[name].shape)
        drawn = base * np.exp(spread * noise) if base else spread * noise
        out[name] = jnp.asarray(drawn.astype(out[name].dtype))
    for name, factor in factors.items():
        out[name] = (out[name] * factor).astype(out[name].dtype)
    return out
```

```python
from contextlib import ExitStack

import concourse.bass as bass
from concourse import mybir

F32 = mybir.dt.float32
F32R = mybir.dt.float32r
I32 = mybir.dt.int32
ALU = mybir.AluOpType
ACT = mybir.ActivationFunctionType
AX = mybir.AxisListType

P = 128
B, T, D = 4, 512, 256
KD = D // P
TT = T // P
H = 16
DH = 64
PAIRS = H // 2
HD = H * DH
BIAS_LEN = 256
MASKED = -1.0e30
M_KEYS = 1601
XD = D // H
E_ROUTED, E_ALL, TOP_K, INTER = 32, 40, 6, 128
ROUTE_SCALE = 2.5
TILES = B * TT
LN_EPS = 1e-5
RMS_EPS = 1.1920928955078125e-07
RSQRT_MAGIC = 0x5F3759DF


class Chain:

    def __init__(self, eng, sem):
        self.eng, self.sem, self.n = eng, sem, 0

    def then_wait(self, ins):
        self.n += 1
        ins.then_inc(self.sem, 1)
        self.eng.wait_ge(self.sem, self.n)


def rsqrt(dve, chain, out, x, tmp, done=None):
    chain.then_wait(dve.tensor_scalar(out.bitcast(I32), x.bitcast(I32), -0.5, float(RSQRT_MAGIC),
                                      ALU.mult, ALU.add))
    for step in range(3):
        chain.then_wait(dve.scalar_tensor_tensor(out=tmp, in0=out, scalar=-0.5, in1=out,
                                                 op0=ALU.mult, op1=ALU.mult))
        chain.then_wait(dve.tensor_tensor(tmp, tmp, x, ALU.mult))
        last = dve.scalar_tensor_tensor(out=out, in0=tmp, scalar=1.5, in1=out,
                                        op0=ALU.add, op1=ALU.mult)
        if step == 2 and done is not None:
            last.then_inc(done, 1)
        else:
            chain.then_wait(last)


def layernorm(dve, chain, out, x, tiles, stats, mean_var, var, rstd, tmp):
    for t in range(tiles):
        last = dve.bn_stats(stats[:, t, :], x[:, t, :])
    chain.then_wait(last)
    for t in range(tiles):
        last = dve.bn_aggr(mean_var[:, t, :], stats[:, t, :])
    chain.then_wait(last)
    chain.then_wait(dve.tensor_scalar(var, mean_var[:, 0:tiles, 1], LN_EPS, None, ALU.add))
    rsqrt(dve, chain, rstd, var, tmp)
    for t in range(tiles):
        last = dve.tensor_scalar(out[:, t, :], x[:, t, :], mean_var[:, t, 0:1], rstd[:, t:t + 1],
                                 ALU.subtract, ALU.mult)
    return last


def self_attention(nc, x, wq, wk, wv, wo, bo, rel_bias, ext_scratch, x1):
    STEPS = H * TT
    PER_PAIR = 2 * TT
    LAG_T = 3
    LAG_PV = LAG_T + 2
    BIAS_W = T + P
    PT_K = (TT - 1) * P
    PT_W = (TT - 1) * (PT_K + P) + P

    with ExitStack() as ctx:
        def sb(name, shape, dt=F32):
            return ctx.enter_context(nc.sbuf_tensor("sa_" + name, shape, dt))

        def bank(name):
            return ctx.enter_context(nc.psum_tensor("sa_" + name, [P, 512], F32))

        sems = []

        def sem(name):
            sems.append(ctx.enter_context(nc.semaphore("sa_" + name)))
            return sems[-1]

        ident = sb("ident", [P, P])
        w_hi = [sb(f"w{n}_hi", [P, KD, HD], F32R) for n in "qkv"]
        w_lo = [sb(f"w{n}_lo", [P, KD, HD], F32R) for n in "qkv"]
        wo_sb = sb("wo", [P, PAIRS, D])
        bo_row = sb("bo", [P, D])
        toeplitz = sb("toeplitz", [P, H, T])
        x_sb = sb("x", [P, TT, D])
        xn = sb("xn", [P, TT, D])
        xt_hi = sb("xt_hi", [P, KD, T], F32R)
        xt_lo = sb("xt_lo", [P, KD, T], F32R)
        v_sb = sb("v", [P, TT, HD])
        q_hi = [[sb(f"q_hi{i}{a}", [P, T], F32R) for a in range(2)] for i in range(2)]
        q_lo = [[sb(f"q_lo{i}{a}", [P, T], F32R) for a in range(2)] for i in range(2)]
        k_hi = [sb(f"k_hi{i}", [P, T], F32R) for i in range(2)]
        k_lo = [sb(f"k_lo{i}", [P, T], F32R) for i in range(2)]
        probs = sb("probs", [P, 4, T])
        pt = sb("pt", [P, 4 * PT_W + TT * P])
        ot = sb("ot", [P, PAIRS, T])
        recip_wide = sb("recip_wide", [P, TT, P])
        recip_bc = sb("recip_bc", [P, T])
        ext = sb("ext", [H, BIAS_W])
        stats = sb("stats", [P, TT, 6])
        mean_var = sb("mean_var", [P, TT, 2])
        var = sb("var", [P, TT])
        rstd = sb("rstd", [P, TT])
        tmp = sb("tmp", [P, TT])
        neg_max = sb("neg_max", [P, STEPS])
        sums = sb("sums", [P, STEPS])
        recip = sb("recip", [P, STEPS])

        pj = [bank(f"pj{i}") for i in range(2)]
        ps = [bank(f"ps{i}") for i in range(2)]
        ptr = [bank(f"ptr{i}") for i in range(2)]
        po = bank("po")
        pr = bank("pr")

        w_in = sem("w_in")
        wo_in = sem("wo_in")
        bias_in = sem("bias_in")
        ext_out = sem("ext_out")
        toep_in = sem("toep_in")
        w_hi_done = sem("w_hi_done")
        ext_done = sem("ext_done")
        zeroed = sem("zeroed")
        prep_done = sem("prep_done")
        raw = [ot[:, 0:4, :], ot[:, 4:8, :], v_sb[:, 0:2, :]]
        raw = [r.rearrange("p a b -> p (a b)") for r in raw]

        with nc.Block() as block:
            @block.sync
            def _(sp):
                sp.dma_start(ext[:, BIAS_LEN:2 * BIAS_LEN], rel_bias).then_inc(bias_in, 16)
                for r, w in zip(raw, (wq, wk, wv)):
                    sp.dma_start(r.rearrange("p (c n) -> p c n", c=KD),
                                 w.rearrange("(c p) n -> p c n", p=P)).then_inc(w_in, 16)
                sp.wait_ge(ext_done, 2)
                for half in range(2):
                    rows = slice(half * H // 2, (half + 1) * H // 2)
                    sp.dma_start(ext_scratch[rows], ext[rows, :].unsqueeze(1)
                                 .to_broadcast([H // 2, P, BIAS_W])).then_inc(ext_out, 16)
                sp.dma_start(wo_sb[:], wo.rearrange("(c p) n -> p c n", p=P)).then_inc(wo_in, 16)
                sp.dma_start(bo_row[:], bo.partition_broadcast(P)).then_inc(wo_in, 16)
                sp.wait_ge(ext_out, 32)
                for h in range(H):
                    sp.dma_start(toeplitz[:, h, :],
                                 bass.AP(ext_scratch.tensor, h * P * BIAS_W + P - 1,
                                         [[BIAS_W - 1, P], [1, T]])).then_inc(toep_in, 16)
                sp.wait_ge(wo_in, 32)
                sp.wait_ge(toep_in, 16 * H)

            @block.gpsimd
            def _(pool):
                pool.memset(ident[:], 0.0).then_inc(zeroed, 1)
                pool.wait_ge(zeroed, 1)
                pool.affine_select(out=ident[:], in_=ident[:], compare_op=ALU.not_equal, fill=1.0,
                                   base=0, pattern=[[-1, P]], channel_multiplier=1
                                   ).then_inc(prep_done, 1)

            @block.scalar
            def _(act):
                act.wait_ge(w_in, 48)
                for r, hi in zip(raw, w_hi):
                    act.activation(hi[:].rearrange("p c n -> p (c n)"), r, ACT.Copy
                                   ).then_inc(w_hi_done, 1)

            @block.vector
            def _(dve):
                dve.memset(ext[:, 2 * BIAS_LEN:], MASKED).then_inc(ext_done, 1)
                dve.wait_ge(bias_in, 16)
                dve.tensor_copy(ext[:, 0:BIAS_LEN],
                                ext[:, BIAS_LEN:BIAS_LEN + 1].to_broadcast([H, BIAS_LEN])
                                ).then_inc(ext_done, 1)
                for i in range(2):
                    for a in range(2):
                        other = slice(DH * (1 - a), DH * (2 - a))
                        dve.memset(q_hi[i][a][other, :].bitcast(F32), 0.0)
                        dve.memset(q_lo[i][a][other, :].bitcast(F32), 0.0)
                for n, (r, hi, lo) in enumerate(zip(raw, w_hi, w_lo)):
                    dve.wait_ge(w_hi_done, n + 1)
                    dve.tensor_tensor(lo[:].rearrange("p c n -> p (c n)"), r,
                                      hi[:].rearrange("p c n -> p (c n)").bitcast(F32),
                                      ALU.subtract).then_inc(prep_done, 1)
        nc.all_engine_barrier(sems_to_clear=range(sems[0].num, sems[-1].num + 1))

        first = len(sems)
        x_in = sem("x_in")
        xn_ready = sem("xn_ready")
        xt_psum = sem("xt_psum")
        xt_hi_ready = sem("xt_hi_ready")
        xt_lo_ready = sem("xt_lo_ready")
        v_psum = sem("v_psum")
        v_even = sem("v_even")
        v_odd = sem("v_odd")
        qk_psum = sem("qk_psum")
        qk_hi_ready = sem("qk_hi_ready")
        qk_lo_ready = sem("qk_lo_ready")
        s_psum = sem("s_psum")
        logits_ready = sem("logits_ready")
        probs_ready = sem("probs_ready")
        pt_psum = sem("pt_psum")
        pt_even = sem("pt_even")
        pt_odd = sem("pt_odd")
        recip_ready = sem("recip_ready")
        recip_wide_ready = sem("recip_wide_ready")
        r_psum = sem("r_psum")
        r_ready = sem("r_ready")
        o_psum = sem("o_psum")
        ot_ready = sem("ot_ready")
        y_psum = sem("y_psum")
        x_bo_ready = sem("x_bo_ready")
        x1_ready = sem("x1_ready")
        x1_out = sem("x1_out")
        dve_chain = sem("dve_chain")
        y_banks = pj + ps

        def tile_of(t):
            h, r = divmod(t, TT)
            return h, r, (r + 1) * P

        def pt_at(h, k, r):
            return (h % 4) * PT_W + k * PT_K + r * P

        def pt_blocks(h, r):
            at = pt_at(h, 0, r)
            return pt[:, at:at + (r + 1) * PT_K].rearrange("p (k c) -> p k c", c=PT_K)[:, :, 0:P]

        def turned(t):
            h, r, w = tile_of(t)
            return ptr[t % 2][:, 0:w].rearrange("p (k c) -> p k c", c=P)

        with nc.Fori(0, B) as b:
            with nc.Block() as block:
                @block.sync
                def _(sp):
                    sp.dma_start(x_sb[:], x[b].rearrange("(t p) d -> p t d", p=P)).then_inc(x_in, 16)
                    sp.wait_ge(x1_ready, TT)
                    sp.dma_start(x1[b].rearrange("(t p) d -> p t d", p=P), xn[:]).then_inc(x1_out, 16)
                    sp.wait_ge(x1_out, 16)

                @block.gpsimd
                def _(pool):
                    pool.wait_ge(xn_ready, 1)
                    for t in range(TT):
                        last = pool.tensor_tensor(x_sb[:, t, :], x_sb[:, t, :], bo_row[:], ALU.add)
                    last.then_inc(x_bo_ready, 1)
                    for p in range(PAIRS):
                        pool.wait_ge(recip_ready, p + 1)
                        if p >= 1:
                            pool.wait_ge(r_psum, p)
                        cols = recip[:, p * PER_PAIR:(p + 1) * PER_PAIR]
                        pool.tensor_copy(recip_wide[:, :, :].rearrange("p r (a d) -> p r a d", a=2),
                                         cols.rearrange("p (a r) -> p r a", a=2).unsqueeze(3)
                                         .to_broadcast([P, TT, 2, DH])).then_inc(recip_wide_ready, 1)

                @block.tensor
                def _(pe):
                    def product(out, parts, chunks):
                        n = 0
                        for c in range(chunks):
                            (a_hi, a_lo), (b_hi, b_lo) = parts(c)
                            for u, v in ((a_hi, b_hi), (a_hi, b_lo), (a_lo, b_hi)):
                                last = pe.matmul(out, u, v, start=(n == 0), stop=(n == 3 * chunks - 1))
                                n += 1
                        return last

                    pe.wait_ge(xn_ready, 1)
                    for c in range(KD):
                        for t in range(TT):
                            last = pe.transpose(ptr[c][:, t * P:(t + 1) * P],
                                                xn[:, t, c * P:(c + 1) * P], ident[:])
                        last.then_inc(xt_psum, 1)
                    pe.wait_ge(xt_lo_ready, KD)
                    for u in range(2 * TT):
                        t, half = divmod(u, 2)
                        if u == 2:
                            pe.wait_ge(v_even, 1)
                        elif u == 3:
                            pe.wait_ge(v_odd, 1)
                        elif u > 3:
                            pe.wait_ge((v_even, v_odd)[u % 2], u // 2)
                        tok, cols = slice(t * P, (t + 1) * P), slice(half * 512, (half + 1) * 512)
                        product(pj[u % 2][:],
                                lambda c: ((xt_hi[:, c, tok], xt_lo[:, c, tok]),
                                           (w_hi[2][:, c, cols], w_lo[2][:, c, cols])), KD
                                ).then_inc(v_psum, 1)

                    def project(p, which):
                        if p == 0:
                            pe.wait_ge((v_even, v_odd)[which], TT)
                        else:
                            pe.wait_ge(qk_lo_ready, 2 * (p - 1) + which + 1)
                        cols = slice(p * P, (p + 1) * P)
                        product(pj[which][:],
                                lambda c: ((w_hi[which][:, c, cols], w_lo[which][:, c, cols]),
                                           (xt_hi[:, c, :], xt_lo[:, c, :])), KD
                                ).then_inc(qk_psum, 1)

                    def scores(t):
                        h, r, w = tile_of(t)
                        p, a = divmod(h, 2)
                        if t % PER_PAIR == 0:
                            pe.wait_ge(qk_lo_ready, 2 * (p + 1))
                        if t >= 2:
                            pe.wait_ge(logits_ready, t - 1)
                        q = slice(r * P, (r + 1) * P)
                        product(ps[t % 2][:, 0:w],
                                lambda c: ((q_hi[p % 2][a][:, q], q_lo[p % 2][a][:, q]),
                                           (k_hi[p % 2][:, 0:w], k_lo[p % 2][:, 0:w])), 1
                                ).then_inc(s_psum, 1)

                    def turn(t):
                        h, r, w = tile_of(t)
                        pe.wait_ge(probs_ready, t + 1)
                        if t >= 2:
                            pe.wait_ge((pt_even, pt_odd)[t % 2], t // 2)
                        for k in range(r + 1):
                            last = pe.transpose(ptr[t % 2][:, k * P:(k + 1) * P],
                                                probs[:, t % 4, k * P:(k + 1) * P], ident[:])
                        last.then_inc(pt_psum, 1)

                    def times_v(p):
                        pe.wait_ge(pt_even, TT * (p + 1))
                        pe.wait_ge(pt_odd, TT * (p + 1))
                        if p >= 1:
                            pe.wait_ge(ot_ready, p)
                        for k in range(TT):
                            for a in range(2):
                                h = 2 * p + a
                                last = pe.matmul(po[a * DH:(a + 1) * DH, k * P:T],
                                                 v_sb[:, k, h * DH:(h + 1) * DH],
                                                 pt[:, pt_at(h, k, k):pt_at(h, k, TT)],
                                                 start=(k == 0), stop=(k == TT - 1))
                        last.then_inc(o_psum, 1)
                        pe.wait_ge(recip_wide_ready, p + 1)
                        for r in range(TT):
                            last = pe.transpose(pr[:, r * P:(r + 1) * P], recip_wide[:, r, :], ident[:])
                        last.then_inc(r_psum, 1)

                    project(0, 0)
                    project(0, 1)
                    for s in range(STEPS + PER_PAIR):
                        if s < STEPS:
                            scores(s)
                        if s % PER_PAIR in (2, 4) and s // PER_PAIR + 1 < PAIRS:
                            project(s // PER_PAIR + 1, s % PER_PAIR // 2 - 1)
                        if LAG_T <= s < STEPS + LAG_T:
                            turn(s - LAG_T)
                        if (s - LAG_PV) % PER_PAIR == PER_PAIR - 1 and s >= LAG_PV:
                            times_v((s - LAG_PV) // PER_PAIR)
                    pe.wait_ge(ot_ready, PAIRS)
                    for t in range(TT):
                        for p in range(PAIRS):
                            last = pe.matmul(y_banks[t][:, 0:D], ot[:, p, t * P:(t + 1) * P],
                                             wo_sb[:, p, :], start=(p == 0), stop=(p == PAIRS - 1))
                        last.then_inc(y_psum, 1)

                @block.scalar
                def _(act):
                    for c in range(KD):
                        act.wait_ge(xt_psum, c + 1)
                        act.activation(xt_hi[:, c, :], ptr[c][:], ACT.Copy).then_inc(xt_hi_ready, 1)
                    for u in range(1, 2 * TT, 2):
                        act.wait_ge(v_psum, u + 1)
                        act.activation(v_sb[:, u // 2, 512:1024], pj[1][:], ACT.Copy
                                       ).then_inc(v_odd, 1)

                    def part_q(p):
                        act.wait_ge(qk_psum, 2 * p + 1)
                        if p >= 2:
                            act.wait_ge(s_psum, PER_PAIR * (p - 1))
                        for a in range(2):
                            rows = slice(a * DH, (a + 1) * DH)
                            last = act.activation(q_hi[p % 2][a][rows, :], pj[0][rows, :], ACT.Copy)
                        last.then_inc(qk_hi_ready, 1)

                    def part_k(p):
                        act.wait_ge(qk_psum, 2 * p + 2)
                        act.activation(k_hi[p % 2][:], pj[1][:], ACT.Copy).then_inc(qk_hi_ready, 1)

                    def exps(t):
                        h, r, w = tile_of(t)
                        act.wait_ge(logits_ready, t + 1)
                        act.activation(probs[:, t % 4, 0:w], probs[:, t % 4, 0:w], ACT.Exp,
                                       bias=neg_max[:, t:t + 1], scale=-1.0,
                                       accum_out=sums[:, t:t + 1]).then_inc(probs_ready, 1)

                    part_q(0)
                    part_k(0)
                    for s in range(STEPS + PER_PAIR):
                        if s < STEPS:
                            exps(s)
                        if s % PER_PAIR == 2 and s // PER_PAIR + 1 < PAIRS:
                            part_q(s // PER_PAIR + 1)
                        if s % PER_PAIR == 4 and s // PER_PAIR + 1 < PAIRS:
                            part_k(s // PER_PAIR + 1)
                        t = s - LAG_T
                        if 0 <= t < STEPS and t % 2 == 1:
                            h, r, w = tile_of(t)
                            act.wait_ge(pt_psum, t + 1)
                            if h >= 4:
                                act.wait_ge(o_psum, (h - 4) // 2 + 1)
                            act.activation(pt_blocks(h, r), turned(t), ACT.Copy).then_inc(pt_odd, 1)
                        if (s - LAG_PV) % PER_PAIR == PER_PAIR - 1 and s >= LAG_PV:
                            p = (s - LAG_PV) // PER_PAIR
                            act.wait_ge(r_psum, p + 1)
                            if p >= 1:
                                act.wait_ge(ot_ready, p)
                            act.activation(recip_bc[:], pr[:], ACT.Copy).then_inc(r_ready, 1)

                @block.vector
                def _(dve):
                    chain = Chain(dve, dve_chain)
                    dve.wait_ge(x_in, 16)
                    layernorm(dve, chain, xn, x_sb, TT, stats, mean_var, var[:], rstd[:], tmp[:]
                              ).then_inc(xn_ready, 1)
                    for c in range(KD):
                        dve.wait_ge(xt_hi_ready, c + 1)
                        dve.tensor_tensor(xt_lo[:, c, :], ptr[c][:], xt_hi[:, c, :].bitcast(F32),
                                          ALU.subtract).then_inc(xt_lo_ready, 1)
                    for u in range(0, 2 * TT, 2):
                        dve.wait_ge(v_psum, u + 1)
                        dve.tensor_copy(v_sb[:, u // 2, 0:512], pj[0][:]).then_inc(v_even, 1)

                    def low_q(p):
                        dve.wait_ge(qk_hi_ready, 2 * p + 1)
                        for a in range(2):
                            rows = slice(a * DH, (a + 1) * DH)
                            last = dve.tensor_tensor(q_lo[p % 2][a][rows, :], pj[0][rows, :],
                                                     q_hi[p % 2][a][rows, :].bitcast(F32), ALU.subtract)
                        last.then_inc(qk_lo_ready, 1)

                    def low_k(p):
                        dve.wait_ge(qk_hi_ready, 2 * p + 2)
                        dve.tensor_tensor(k_lo[p % 2][:], pj[1][:], k_hi[p % 2][:].bitcast(F32),
                                          ALU.subtract).then_inc(qk_lo_ready, 1)

                    def biased(t):
                        h, r, w = tile_of(t)
                        dve.wait_ge(s_psum, t + 1)
                        if t >= 4:
                            dve.wait_ge(pt_psum, t - 3)
                        dve.tensor_tensor_reduce(out=probs[:, t % 4, 0:w], in0=ps[t % 2][:, 0:w],
                                                 in1=toeplitz[:, h, T - w:T], scale=-1.0 / DH,
                                                 scalar=3.0e38, op0=ALU.add, op1=ALU.min,
                                                 accum_out=neg_max[:, t:t + 1]
                                                 ).then_inc(logits_ready, 1)

                    low_q(0)
                    low_k(0)
                    for s in range(STEPS + PER_PAIR):
                        if s < STEPS:
                            biased(s)
                        if s % PER_PAIR == 2 and s // PER_PAIR + 1 < PAIRS:
                            low_q(s // PER_PAIR + 1)
                        if s % PER_PAIR == 4 and s // PER_PAIR + 1 < PAIRS:
                            low_k(s // PER_PAIR + 1)
                        t = s - LAG_T
                        if 0 <= t < STEPS and t % 2 == 0:
                            h, r, w = tile_of(t)
                            dve.wait_ge(pt_psum, t + 1)
                            if h >= 4:
                                dve.wait_ge(o_psum, (h - 4) // 2 + 1)
                            dve.tensor_copy(pt_blocks(h, r), turned(t)).then_inc(pt_even, 1)
                        if t % PER_PAIR == PER_PAIR - 1 and 0 <= t < STEPS:
                            p = t // PER_PAIR
                            dve.wait_ge(probs_ready, PER_PAIR * (p + 1))
                            cols = slice(p * PER_PAIR, (p + 1) * PER_PAIR)
                            dve.reciprocal(recip[:, cols], sums[:, cols]).then_inc(recip_ready, 1)
                        if (s - LAG_PV) % PER_PAIR == PER_PAIR - 1 and s >= LAG_PV:
                            p = (s - LAG_PV) // PER_PAIR
                            dve.wait_ge(o_psum, p + 1)
                            dve.wait_ge(r_ready, p + 1)
                            dve.tensor_tensor(ot[:, p, :], po[:], recip_bc[:], ALU.mult
                                              ).then_inc(ot_ready, 1)
                    dve.wait_ge(x_bo_ready, 1)
                    for t in range(TT):
                        dve.wait_ge(y_psum, t + 1)
                        dve.tensor_tensor(xn[:, t, :], y_banks[t][:, 0:D], x_sb[:, t, :], ALU.add
                                          ).then_inc(x1_ready, 1)
            nc.all_engine_barrier(sems_to_clear=range(sems[first].num, sems[-1].num + 1))


def cross_attention(nc, x1, ctx_t, wq_t, bq, wkv_t, bkv, q_gamma, k_gamma, x2):
    SAFE = 40.0
    SLOT = 4 * XD
    SHIFT = 3 * XD
    QUADS = H // 4
    KT = -(-M_KEYS // P)
    GROUPS = [(0, 4), (4, 8), (8, 12), (12, KT)]
    ENDS = [hi - 1 for lo, hi in GROUPS]
    CUT_AFTER = [hi - 1 for lo, hi in GROUPS[:-2]]
    LAG_K = 6
    UNITS = QUADS * KT * 2
    DEEP = 3
    RING = 6
    LAG = 4
    SPAN = 402
    SPAN_AT = [0, 400, 800, M_KEYS - SPAN]

    with ExitStack() as ctx:
        def sb(name, shape, dt=F32):
            return ctx.enter_context(nc.sbuf_tensor("xa_" + name, shape, dt))

        sems = []

        def sem(name):
            sems.append(ctx.enter_context(nc.semaphore("xa_" + name)))
            return sems[-1]

        ident = sb("ident", [P, P])
        wq_sb = sb("wq", [P, KD, D])
        wkv_hi = sb("wkv_hi", [P, KD, 2 * D], F32R)
        wkv_lo = sb("wkv_lo", [P, KD, 2 * D], F32R)
        bq_row = sb("bq", [P, D])
        bkv_row = sb("bkv", [P, 2 * D])
        gammas = sb("gammas", [P, 2, XD])
        gain = sb("gain", [P, XD])
        bound = sb("bound", [P, 1])
        unsafe = sb("unsafe", [P, 1], I32)
        x_sb = sb("x", [P, TT, D])
        xn = sb("xn", [P, TT, D])
        q_tok = sb("q_tok", [P, TT, H, SLOT], F32R)
        q_aug = sb("q_aug", [P, H, T], F32R)
        k_tok = [sb(f"k_tok{i}", [P, H, SLOT], F32R) for i in range(2)]
        k_aug = sb("k_aug", [P, PAIRS, M_KEYS + 1], F32R)
        v_one = sb("v_one", [P, KT, H, XD + 1])
        maxima = sb("maxima", [P, H, TT, 2])
        stats = sb("stats", [P, TT, 6])
        mean_var = sb("mean_var", [P, TT, 2])
        var = sb("var", [P, TT])
        rstd = sb("rstd", [P, TT])
        tmp = sb("tmp", [P, TT])
        square_sum = sb("square_sum", [P, 4 * H])
        rms = sb("rms", [P, 4 * H])
        rms_q = sb("rms_q", [P, 4 * H])
        rms_tmp = sb("rms_tmp", [P, 4 * H])

        outer = ctx
        with ExitStack() as ctx:
            xt = sb("xt", [P, KD, T])
            qb = sb("qb", [P, TT, D])
            raw = [sb(f"raw{i}", [P, KD, 4 * P]) for i in range(2)]
            ct_hi = [sb(f"ct_hi{i}", [P, KD, 4 * P], F32R) for i in range(2)]
            ct_lo = [sb(f"ct_lo{i}", [P, KD, 4 * P], F32R) for i in range(2)]
            kb = [sb(f"kb{i}", [P, 4, D]) for i in range(2)]
            sq = [sb(f"sq{i}", [P, 4, D]) for i in range(2)]
        ctx = outer
        probs = sb("probs", [P, RING, 2, T])
        o_sb = [sb(f"o{i}", [P, T]) for i in range(2)]
        o_norm = sb("o_norm", [P, TT, 4, XD])
        rec = sb("rec", [P, TT, 4])

        banks = ctx.enter_context(nc.psum_tensor("xa_banks", [P, 8, 512], F32))

        w_in = sem("w_in")
        wkv_in = sem("wkv_in")
        gain_done = sem("gain_done")
        hi_done = sem("hi_done")
        zeroed = sem("zeroed")
        set_chain = sem("set_chain")

        with nc.Block() as block:
            @block.sync
            def _(sp):
                sp.dma_start(raw[0][:], wkv_t.rearrange("(c p) n -> p c n", p=P)).then_inc(wkv_in, 16)
                sp.dma_start(wq_sb[:], wq_t.rearrange("(c p) n -> p c n", p=P)).then_inc(w_in, 16)
                sp.dma_start(bq_row[:], bq.partition_broadcast(P)).then_inc(w_in, 16)
                sp.dma_start(bkv_row[:], bkv.partition_broadcast(P)).then_inc(w_in, 16)
                sp.dma_start(gammas[:, 0, :], q_gamma.partition_broadcast(P)).then_inc(w_in, 16)
                sp.dma_start(gammas[:, 1, :], k_gamma.partition_broadcast(P)).then_inc(w_in, 16)
                sp.wait_ge(w_in, 80)

            @block.gpsimd
            def _(pool):
                pool.memset(ident[:], 0.0).then_inc(zeroed, 1)
                pool.wait_ge(zeroed, 1)
                pool.affine_select(out=ident[:], in_=ident[:], compare_op=ALU.not_equal, fill=1.0,
                                   base=0, pattern=[[-1, P]], channel_multiplier=1)
                pool.memset(v_one[:, :, :, XD:XD + 1], 1.0)

            @block.scalar
            def _(act):
                act.wait_ge(wkv_in, 16)
                act.activation(wkv_hi[:], raw[0][:], ACT.Copy).then_inc(hi_done, 1)

            @block.vector
            def _(dve):
                chain = Chain(dve, set_chain)
                for k in k_tok:
                    dve.memset(k[:].bitcast(F32), 0.0)
                last = dve.memset(q_tok[:].bitcast(F32), 0.0)
                chain.then_wait(last)
                for k in k_tok:
                    dve.memset(k[:, :, SHIFT:SHIFT + 1].bitcast(F32), 1.0)
                for a in range(2):
                    rest = q_aug[SLOT * (1 - a):SLOT * (2 - a), a:H:2, :]
                    dve.memset(rest.bitcast(F32), 0.0)
                dve.memset(banks[:, 6, :], 0.0)
                dve.wait_ge(w_in, 80)
                chain.then_wait(dve.tensor_tensor(gain[:], gammas[:, 0, :], gammas[:, 1, :], ALU.mult))
                chain.then_wait(dve.tensor_reduce(bound[:], gain[:], AX.X, ALU.max,
                                                  apply_absolute_value=True))
                chain.then_wait(dve.tensor_scalar(unsafe[:], bound[:], SAFE / 4.0, None, ALU.is_gt))
                dve.tensor_scalar(gain[:], gain[:], float(XD) ** -0.5, None, ALU.mult
                                  ).then_inc(gain_done, 1)
                dve.wait_ge(hi_done, 1)
                dve.tensor_tensor(wkv_lo[:], raw[0][:], wkv_hi[:].bitcast(F32), ALU.subtract)
        nc.all_engine_barrier(sems_to_clear=range(sems[0].num, sems[-1].num + 1))

        first = len(sems)
        x_in = sem("x_in")
        ctx_in = [sem("ctx_in0"), sem("ctx_in1")]
        xn_ready = sem("xn_ready")
        xt_psum = sem("xt_psum")
        xt_ready = sem("xt_ready")
        q_psum = sem("q_psum")
        q_biased = sem("q_biased")
        q_hi_ready = sem("q_hi_ready")
        q_tok_ready = sem("q_tok_ready")
        qt_psum = sem("qt_psum")
        q_aug_a = sem("q_aug_a")
        q_aug_b = sem("q_aug_b")
        ct_hi_ready = sem("ct_hi_ready")
        ct_lo_ready = sem("ct_lo_ready")
        kv_psum = sem("kv_psum")
        kb_ready = sem("kb_ready")
        v_ready = sem("v_ready")
        sq_ready = sem("sq_ready")
        rms_ready = sem("rms_ready")
        kn_ready = sem("kn_ready")
        k_hi_ready = sem("k_hi_ready")
        k_tok_ready = sem("k_tok_ready")
        kt_psum = sem("kt_psum")
        k_aug_a = sem("k_aug_a")
        k_aug_b = sem("k_aug_b")
        max_psum = sem("max_psum")
        max_ready = sem("max_ready")
        shift_ready = sem("shift_ready")
        qt2_psum = sem("qt2_psum")
        q2_aug_a = sem("q2_aug_a")
        q2_aug_b = sem("q2_aug_b")
        s_psum = sem("s_psum")
        probs_ready = sem("probs_ready")
        pv_done = sem("pv_done")
        o_psum = sem("o_psum")
        o_ready = sem("o_ready")
        ot_psum = sem("ot_psum")
        o_norm_ready = sem("o_norm_ready")
        x_bv_ready = sem("x_bv_ready")
        x2_part = sem("x2_part")
        x2_out = sem("x2_out")
        dve_chain = sem("dve_chain")

        def rows_of(c):
            return min(P, M_KEYS - c * P)

        def unit(n):
            g, rest = divmod(n, 2 * KT)
            return g, rest // 2, rest % 2, rows_of(rest // 2)

        with nc.Fori(0, B) as b:
            with nc.Block() as block:
                @block.sync
                def _(sp):
                    for g, (lo, hi) in enumerate(GROUPS):
                        n = min(M_KEYS, hi * P) - lo * P
                        if g >= 2:
                            sp.wait_ge(ct_lo_ready, g - 1)
                        sp.dma_start(raw[g % 2][:, :, 0:n],
                                     ctx_t[b].rearrange("(c p) m -> p c m", p=P)[:, :, lo * P:lo * P + n]
                                     ).then_inc(ctx_in[g % 2], 16)
                        if g == 0:
                            sp.dma_start(x_sb[:], x1[b].rearrange("(t p) d -> p t d", p=P)
                                         ).then_inc(x_in, 16)
                    sp.wait_ge(x2_part, QUADS)
                    sp.dma_start(x2[b].rearrange("(t p) d -> p t d", p=P), x_sb[:]).then_inc(x2_out, 16)
                    sp.wait_ge(x2_out, 16)

                @block.gpsimd
                def _(pool):
                    pool.wait_ge(xn_ready, 1)
                    pool.tensor_tensor(x_sb[:], x_sb[:],
                                       bkv_row[:, D:2 * D].unsqueeze(1).to_broadcast([P, TT, D]),
                                       ALU.add).then_inc(x_bv_ready, 1)
                    for g, (lo, hi) in enumerate(GROUPS):
                        for c in range(lo, hi):
                            m, i = rows_of(c), c % 4
                            pool.wait_ge(kb_ready, c + 1)
                            pool.tensor_tensor(sq[g % 2][0:m, i, :], kb[g % 2][0:m, i, :], kb[g % 2][0:m, i, :], ALU.mult
                                               ).then_inc(sq_ready, 1)
                        pool.wait_ge(rms_ready, g + 1)
                        for c in range(lo, hi):
                            m, i = rows_of(c), c % 4
                            pool.tensor_tensor(
                                sq[g % 2][0:m, i, :].rearrange("p (h d) -> p h d", h=H),
                                kb[g % 2][0:m, i, :].rearrange("p (h d) -> p h d", h=H),
                                rms[0:m, i * H:(i + 1) * H].unsqueeze(2).to_broadcast([m, H, XD]),
                                ALU.mult).then_inc(kn_ready, 1)
                    pool.wait_ge(x_bv_ready, 1)
                    for g in range(QUADS):
                        pool.wait_ge(o_norm_ready, g + 1)
                        cols = x_sb[:, :, g * 4 * XD:(g + 1) * 4 * XD]
                        pool.tensor_tensor(cols, cols, o_norm[:].rearrange("p t j d -> p t (j d)"),
                                           ALU.add).then_inc(x2_part, 1)

                @block.tensor
                def _(pe):
                    def turn_k(c):
                        m = rows_of(c)
                        pe.wait_ge(k_tok_ready, c + 1)
                        if c >= 2:
                            pe.wait_ge(k_aug_a, c - 1)
                            pe.wait_ge(k_aug_b, c - 1)
                        for p in range(PAIRS):
                            out = banks[:, 2 + 2 * (c % 2) + p // 4, (p % 4) * P:(p % 4) * P + m]
                            last = pe.transpose(
                                out, k_tok[c % 2][0:m, 2 * p:2 * p + 2, :].bitcast(F32)
                                .rearrange("p h d -> p (h d)"), ident[0:m, 0:m])
                        last.then_inc(kt_psum, 1)

                    def keys_values(c):
                        m, g, i = rows_of(c), c // 4, c % 4
                        if i == 0:
                            pe.wait_ge(ct_lo_ready, g + 1)
                        if c >= 2:
                            pe.wait_ge(kb_ready, c - 1)
                            pe.wait_ge(v_ready, c - 1)
                        n = 0
                        for k in range(KD):
                            for u, w in ((ct_hi, wkv_hi), (ct_hi, wkv_lo), (ct_lo, wkv_hi)):
                                last = pe.matmul(banks[0:m, c % 2, :],
                                                 u[g % 2][:, k, i * P:i * P + m], w[:, k, :],
                                                 start=(n == 0), stop=(n == 3 * KD - 1))
                                n += 1
                        last.then_inc(kv_psum, 1)

                    def turn_x():
                        pe.wait_ge(xn_ready, 1)
                        for c in range(KD):
                            for t in range(TT):
                                last = pe.transpose(banks[:, 6 + c, t * P:(t + 1) * P],
                                                    xn[:, t, c * P:(c + 1) * P], ident[:])
                            last.then_inc(xt_psum, 1)

                    def project_q():
                        pe.wait_ge(xt_ready, KD)
                        for t in range(TT):
                            for c in range(KD):
                                last = pe.matmul(banks[:, 6 + t // 2, (t % 2) * D:(t % 2 + 1) * D],
                                                 xt[:, c, t * P:(t + 1) * P],
                                                 wq_sb[:, c, :], start=(c == 0), stop=(c == KD - 1))
                            if t % 2 == 1:
                                last.then_inc(q_psum, 1)

                    for step in range(KT + LAG_K):
                        if step < KT:
                            keys_values(step)
                        if step >= LAG_K:
                            turn_k(step - LAG_K)
                        if step == 3:
                            turn_x()
                        if step == 7:
                            project_q()

                    def turn_q(done, after_a, after_b):
                        for p in range(PAIRS):
                            if p >= 2:
                                pe.wait_ge(after_a, p - 1)
                                pe.wait_ge(after_b, p - 1)
                            for t in range(TT):
                                last = pe.transpose(
                                    banks[:, 6 + p % 2, t * P:(t + 1) * P],
                                    q_tok[:, t, 2 * p:2 * p + 2, :].bitcast(F32)
                                    .rearrange("p h d -> p (h d)"), ident[:])
                            last.then_inc(done, 1)
                        pe.wait_ge(after_a, PAIRS)
                        pe.wait_ge(after_b, PAIRS)

                    pe.wait_ge(q_tok_ready, 1)
                    turn_q(qt_psum, q_aug_a, q_aug_b)
                    pe.wait_ge(k_aug_a, KT)
                    pe.wait_ge(k_aug_b, KT)
                    with pe.If(pe.value_load(unsafe[0:1, 0:1], min_val=0, max_val=1) > 0):
                        for n in range(2 * H * TT):
                            h, t, half = n // (2 * TT), n // 2 % TT, n % 2
                            if n >= 2:
                                pe.wait_ge(max_ready, n - 1)
                            for i in range(2):
                                at = SPAN_AT[2 * half + i]
                                last = pe.matmul(banks[:, 2 * (n % 2) + i, 0:SPAN],
                                                 q_aug[:, h, t * P:(t + 1) * P],
                                                 k_aug[:, h // 2, at:at + SPAN], start=True, stop=True)
                            last.then_inc(max_psum, 1)
                        pe.wait_ge(shift_ready, 1)
                        turn_q(qt2_psum, q2_aug_a, q2_aug_b)
                    with pe.Else():
                        pe.nop()

                    def scores(n):
                        g, c, half, m = unit(n)
                        if n >= DEEP:
                            pe.wait_ge(probs_ready, n - DEEP + 1)
                        for i in range(2):
                            h = 4 * g + 2 * half + i
                            last = pe.matmul(banks[0:m, 2 * (n % DEEP) + i, :],
                                             k_aug[:, h // 2, c * P:c * P + m], q_aug[:, h, :],
                                             start=True, stop=True)
                        last.then_inc(s_psum, 1)

                    def times_v(n):
                        g, c, half, m = unit(n)
                        pe.wait_ge(probs_ready, n + 1)
                        if c == 0 and g >= 1:
                            pe.wait_ge(o_ready, g)
                        for j in range(4):
                            last = pe.matmul(banks[32 * j:32 * j + XD + 1, 6, :],
                                             v_one[0:m, c, 4 * g + j, :],
                                             probs[0:m, (n - 1 + j // 2) % RING, j % 2, :],
                                             start=(c == 0), stop=(c == KT - 1))
                        last.then_inc(pv_done, 1)
                        if c == KT - 1:
                            turn_o.append(g)

                    def turn_heads(g):
                        pe.wait_ge(o_ready, g + 1)
                        if g >= 1:
                            pe.wait_ge(o_norm_ready, g)
                        for t in range(TT):
                            last = pe.transpose(banks[:, 7, t * P:(t + 1) * P],
                                                o_sb[g % 2][:, t * P:(t + 1) * P], ident[:])
                        last.then_inc(ot_psum, 1)

                    turn_o = []
                    for s in range(UNITS + LAG):
                        if s < UNITS:
                            scores(s)
                        if s % (2 * KT) == LAG + 6 and turn_o:
                            turn_heads(turn_o.pop())
                        if s >= LAG and (s - LAG) % 2 == 1:
                            times_v(s - LAG)
                    turn_heads(turn_o.pop())

                @block.scalar
                def _(act):
                    def cut(g):
                        lo, hi = GROUPS[g]
                        n = min(M_KEYS, hi * P) - lo * P
                        act.wait_ge(ctx_in[g % 2], 16 * (g // 2 + 1))
                        if g >= 2:
                            act.wait_ge(kv_psum, GROUPS[g - 2][1])
                        act.activation(ct_hi[g % 2][:, :, 0:n], raw[g % 2][:, :, 0:n], ACT.Copy
                                       ).then_inc(ct_hi_ready, 1)

                    def move_k(c):
                        m = rows_of(c)
                        act.wait_ge(kt_psum, c + 1)
                        act.activation(k_aug[:, 0:4, c * P:c * P + m],
                                       banks[:, 2 + 2 * (c % 2), :].rearrange("p (a k) -> p a k", a=4)
                                       [:, :, 0:m], ACT.Copy).then_inc(k_aug_a, 1)

                    def move_v(c):
                        m = rows_of(c)
                        act.wait_ge(kb_ready, c + 1)
                        act.activation(v_one[0:m, c, :, 0:XD],
                                       banks[0:m, c % 2, D:2 * D].rearrange("p (h d) -> p h d", h=H),
                                       ACT.Copy).then_inc(v_ready, 1)

                    def high_k(c):
                        m = rows_of(c)
                        act.wait_ge(kn_ready, c + 1)
                        if c >= 2:
                            act.wait_ge(kt_psum, c - 1)
                        slots = k_tok[c % 2][0:m, :, :].rearrange("p h (s d) -> p h s d", s=4)
                        act.activation(slots[:, :, 0:3:2, :],
                                       sq[c // 4 % 2][0:m, c % 4, :]
                                       .rearrange("p (h d) -> p h d", h=H).unsqueeze(2)
                                       .to_broadcast([m, H, 2, XD]), ACT.Copy
                                       ).then_inc(k_hi_ready, 1)

                    def move_x():
                        for c in range(KD):
                            act.wait_ge(xt_psum, c + 1)
                            act.activation(xt[:, c, :], banks[:, 6 + c, :], ACT.Copy
                                           ).then_inc(xt_ready, 1)

                    def high_q():
                        act.wait_ge(q_biased, TT + 1)
                        for t in range(TT):
                            last = act.activation(
                                q_tok[:, t, :, 0:2 * XD].rearrange("p h (s d) -> p h s d", s=2),
                                qb[:, t, :].rearrange("p (h d) -> p h d", h=H).unsqueeze(2)
                                .to_broadcast([P, H, 2, XD]), ACT.Copy)
                        last.then_inc(q_hi_ready, 1)

                    cut(0)
                    cut(1)
                    for step in range(KT + LAG_K):
                        if step >= LAG_K:
                            high_k(step - LAG_K)
                        if step < KT:
                            move_v(step)
                        if step > LAG_K:
                            move_k(step - LAG_K - 1)
                        if step == 3:
                            move_x()
                        if step == 11:
                            high_q()
                        if step in CUT_AFTER:
                            cut(2 + CUT_AFTER.index(step))
                    move_k(KT - 1)

                    def evacuate_q(done, ready):
                        for p in range(PAIRS):
                            act.wait_ge(done, p + 1)
                            act.activation(q_aug[0:SLOT, 2 * p, :], banks[0:SLOT, 6 + p % 2, :], ACT.Copy
                                           ).then_inc(ready, 1)

                    evacuate_q(qt_psum, q_aug_a)
                    with act.If(act.value_load(unsafe[0:1, 0:1], min_val=0, max_val=1) > 0):
                        evacuate_q(qt2_psum, q2_aug_a)
                    with act.Else():
                        act.nop()
                    for n in range(UNITS):
                        g, c, half, m = unit(n)
                        act.wait_ge(s_psum, n + 1)
                        if n >= RING:
                            act.wait_ge(pv_done, (n - RING) // 2 + 1)
                        act.activation(probs[0:m, n % RING, :, :],
                                       banks[0:m, 2 * (n % DEEP):2 * (n % DEEP) + 2, :], ACT.Exp
                                       ).then_inc(probs_ready, 1)

                @block.vector
                def _(dve):
                    chain = Chain(dve, dve_chain)
                    def cut(g):
                        lo, hi = GROUPS[g]
                        n = min(M_KEYS, hi * P) - lo * P
                        dve.wait_ge(ct_hi_ready, g + 1)
                        dve.tensor_tensor(ct_lo[g % 2][:, :, 0:n], raw[g % 2][:, :, 0:n],
                                          ct_hi[g % 2][:, :, 0:n].bitcast(F32), ALU.subtract
                                          ).then_inc(ct_lo_ready, 1)

                    cut(0)
                    dve.wait_ge(x_in, 16)
                    layernorm(dve, chain, xn, x_sb, TT, stats, mean_var, var[:], rstd[:], tmp[:]
                              ).then_inc(xn_ready, 1)
                    cut(1)

                    def rms_norm(x, tiles, m, rms, done=None):
                        n = tiles * H
                        chain.then_wait(dve.tensor_reduce(
                            square_sum[0:m, 0:n], x.rearrange("p t (h d) -> p (t h) d", h=H), AX.X, ALU.add))
                        chain.then_wait(dve.tensor_scalar(square_sum[0:m, 0:n], square_sum[0:m, 0:n],
                                                          1.0 / XD, RMS_EPS, ALU.mult, ALU.add))
                        rsqrt(dve, chain, rms[0:m, 0:n], square_sum[0:m, 0:n], rms_tmp[0:m, 0:n], done)

                    def add_bias(c):
                        m = rows_of(c)
                        dve.wait_ge(kv_psum, c + 1)
                        dve.tensor_tensor(kb[c // 4 % 2][0:m, c % 4, :], banks[0:m, c % 2, 0:D],
                                          bkv_row[0:m, 0:D], ALU.add).then_inc(kb_ready, 1)

                    def low_k(c):
                        m = rows_of(c)
                        dve.wait_ge(k_hi_ready, c + 1)
                        dve.tensor_tensor(k_tok[c % 2][0:m, :, XD:2 * XD],
                                          sq[c // 4 % 2][0:m, c % 4, :]
                                          .rearrange("p (h d) -> p h d", h=H),
                                          k_tok[c % 2][0:m, :, 0:XD].bitcast(F32), ALU.subtract
                                          ).then_inc(k_tok_ready, 1)

                    def move_k(c):
                        m = rows_of(c)
                        dve.wait_ge(kt_psum, c + 1)
                        dve.tensor_copy(k_aug[:, 4:8, c * P:c * P + m],
                                        banks[:, 3 + 2 * (c % 2), :].rearrange("p (a k) -> p a k", a=4)
                                        [:, :, 0:m]).then_inc(k_aug_b, 1)

                    def normalise_q():
                        for n in range(2):
                            dve.wait_ge(q_psum, n + 1)
                            dve.tensor_tensor(qb[:, 2 * n:2 * n + 2, :],
                                              banks[:, 6 + n, :].rearrange("p (t d) -> p t d", t=2),
                                              bq_row[:].unsqueeze(1).to_broadcast([P, 2, D]), ALU.add
                                              ).then_inc(q_biased, TT // 2)
                        dve.wait_ge(q_biased, TT)
                        chain.then_wait(dve.tensor_tensor(xn[:], qb[:], qb[:], ALU.mult))
                        rms_norm(xn[:], TT, P, rms_q)
                        heads = qb[:].rearrange("p t (h d) -> p (t h) d", h=H)
                        chain.then_wait(dve.tensor_tensor(
                            heads, heads, rms_q[:].unsqueeze(2).to_broadcast([P, TT * H, XD]), ALU.mult))
                        dve.tensor_tensor(heads, heads, gain[:].unsqueeze(1)
                                          .to_broadcast([P, TT * H, XD]), ALU.mult
                                          ).then_inc(q_biased, 1)

                    def low_q():
                        dve.memset(q_tok[:, :, :, SHIFT:SHIFT + 1].bitcast(F32), 0.0)
                        dve.wait_ge(q_hi_ready, 1)
                        for t in range(TT):
                            last = dve.tensor_tensor(q_tok[:, t, :, 2 * XD:3 * XD],
                                                     qb[:, t, :].rearrange("p (h d) -> p h d", h=H),
                                                     q_tok[:, t, :, 0:XD].bitcast(F32), ALU.subtract)
                        last.then_inc(q_tok_ready, 1)

                    for step in range(KT + LAG_K):
                        if step >= LAG_K:
                            low_k(step - LAG_K)
                        if step < KT:
                            add_bias(step)
                        if step > LAG_K:
                            move_k(step - LAG_K - 1)
                        if step < KT and step in ENDS:
                            g = ENDS.index(step)
                            lo, hi = GROUPS[g]
                            dve.wait_ge(sq_ready, hi)
                            if g >= 1:
                                dve.wait_ge(kn_ready, lo)
                            rms_norm(sq[g % 2][0:rows_of(lo), 0:hi - lo, :], hi - lo, rows_of(lo),
                                     rms, rms_ready)
                        if step == 8:
                            normalise_q()
                        if step == 12:
                            low_q()
                        if step in CUT_AFTER:
                            cut(2 + CUT_AFTER.index(step))
                    move_k(KT - 1)

                    def evacuate_q(done, ready):
                        for p in range(PAIRS):
                            dve.wait_ge(done, p + 1)
                            dve.tensor_copy(q_aug[SLOT:P, 2 * p + 1, :], banks[SLOT:P, 6 + p % 2, :]
                                            ).then_inc(ready, 1)

                    evacuate_q(qt_psum, q_aug_b)
                    with dve.If(dve.value_load(unsafe[0:1, 0:1], min_val=0, max_val=1) > 0):
                        for n in range(2 * H * TT):
                            h, t, half = n // (2 * TT), n // 2 % TT, n % 2
                            dve.wait_ge(max_psum, n + 1)
                            last = dve.tensor_reduce(maxima[:, h, t, half:half + 1],
                                                     banks[:, 2 * (n % 2):2 * (n % 2) + 2, 0:SPAN],
                                                     AX.XY, ALU.max)
                            last.then_inc(max_ready, 1)
                        dve.wait_ge(max_ready, 2 * H * TT)
                        for t in range(TT):
                            last = dve.tensor_reduce(q_tok[:, t, :, SHIFT:SHIFT + 1], maxima[:, :, t, :],
                                                     AX.X, ALU.max, negate=True)
                        last.then_inc(shift_ready, 1)
                        evacuate_q(qt2_psum, q2_aug_b)
                    with dve.Else():
                        dve.nop()
                    for g in range(QUADS):
                        dve.wait_ge(pv_done, KT * (g + 1))
                        dve.tensor_copy(o_sb[g % 2][:], banks[:, 6, :]).then_inc(o_ready, 1)
                        dve.wait_ge(ot_psum, g + 1)
                        heads = banks[:, 7, :].rearrange("p (t j d) -> p t j d", t=TT, j=4)
                        chain.then_wait(dve.reciprocal(rec[:], heads[:, :, :, XD:XD + 1]
                                                       .rearrange("p t j d -> p t (j d)")))
                        if g >= 1:
                            dve.wait_ge(x2_part, g)
                        dve.tensor_tensor(o_norm[:], heads[:, :, :, 0:XD],
                                          rec[:].unsqueeze(3).to_broadcast([P, TT, 4, XD]), ALU.mult
                                          ).then_inc(o_norm_ready, 1)
            nc.all_engine_barrier(sems_to_clear=range(sems[first].num, sems[-1].num + 1))


def experts(nc, x2, cls_t, score_bias, gate_up_t, down_t, out):
    CHUNKS = B * T // 512
    PER_TURN = 2 * CHUNKS
    TURNS = E_ROUTED // 2
    SENTINELS = 2
    HUGE = 3.0e38

    with ExitStack() as ctx:
        def sb(name, shape, dt=F32):
            return ctx.enter_context(nc.sbuf_tensor("mo_" + name, shape, dt))

        sems = []

        def sem(name):
            sems.append(ctx.enter_context(nc.semaphore("mo_" + name)))
            return sems[-1]

        ident = sb("ident", [P, P])
        acc = sb("acc", [P, TILES, D])
        xn = sb("xn", [P, TILES, D])
        xt_hi = sb("xt_hi", [P, KD, B * T], F32R)
        xt_lo = sb("xt_lo", [P, KD, B * T], F32R)
        cls = sb("cls", [P, KD, E_ALL])
        cls_hi = sb("cls_hi", [P, KD, E_ALL], F32R)
        cls_lo = sb("cls_lo", [P, KD, E_ALL], F32R)
        bias_row = sb("bias_row", [P, E_ALL])
        stats = sb("stats", [P, TILES, 6])
        mean_var = sb("mean_var", [P, TILES, 2])
        var = sb("var", [P, TILES])
        rstd = sb("rstd", [P, TILES])
        tmp = sb("tmp", [P, TILES])
        scores = sb("scores", [P, TILES, E_ALL])
        choice = sb("choice", [P, TILES, E_ALL + SENTINELS])
        left = sb("left", [P, TILES, E_ALL + SENTINELS])
        top = sb("top", [P, TILES, 8])
        weights = sb("weights", [P, E_ALL, TILES])
        current = [sb(f"current{i}", [P, TILES]) for i in range(2)]
        zero_w = sb("zero_w", [P, TILES])
        gu_raw = [sb(f"gu_raw{i}", [P, KD, 2 * INTER]) for i in range(2)]
        dn_raw = [sb(f"dn_raw{i}", [P, D]) for i in range(2)]
        gu_hi = [sb(f"gu_hi{i}", [P, KD, 2 * INTER], F32R) for i in range(2)]
        gu_lo = [sb(f"gu_lo{i}", [P, KD, 2 * INTER], F32R) for i in range(2)]
        dn_hi = [sb(f"dn_hi{i}", [P, D], F32R) for i in range(2)]
        dn_lo = [sb(f"dn_lo{i}", [P, D], F32R) for i in range(2)]
        silu = [sb(f"silu{i}", [P, 512]) for i in range(2)]
        hidden = [sb(f"hidden{i}", [P, 512]) for i in range(2)]
        h_hi = [sb(f"h_hi{i}", [P, 512], F32R) for i in range(2)]
        h_lo = [sb(f"h_lo{i}", [P, 512], F32R) for i in range(2)]
        banks = ctx.enter_context(nc.psum_tensor("mo_banks", [P, 8, 512], F32))

        x_in = sem("x_in")
        router_in = sem("router_in")
        zeroed = sem("zeroed")
        ident_ready = sem("ident_ready")
        cls_ready = sem("cls_ready")
        xn_ready = sem("xn_ready")
        xt_psum = sem("xt_psum")
        xt_hi_ready = sem("xt_hi_ready")
        xt_lo_ready = sem("xt_lo_ready")
        logits_psum = sem("logits_psum")
        shifted = sem("shifted")
        exp_ready = sem("exp_ready")
        dve_chain = sem("dve_chain")
        gu_in = [sem("gu_in0"), sem("gu_in1")]
        w_hi_ready = sem("w_hi_ready")
        w_ready = sem("w_ready")
        gu_psum = sem("gu_psum")
        silu_ready = sem("silu_ready")
        h_ready = sem("h_ready")
        h_hi_ready = sem("h_hi_ready")
        h_lo_ready = sem("h_lo_ready")
        y_psum = sem("y_psum")
        y_added = sem("y_added")
        current_ready = sem("current_ready")
        out_done = sem("out_done")

        with nc.Block() as block:
            @block.sync
            def _(sp):
                x2_v = x2.rearrange("b (t p) d -> p (b t) d", p=P)
                for g in range(B):
                    sp.dma_start(acc[:, TT * g:TT * g + TT, :], x2_v[:, TT * g:TT * g + TT, :]
                                 ).then_inc(x_in, 16)
                sp.dma_start(cls[:], cls_t.rearrange("(c p) e -> p c e", p=P)).then_inc(router_in, 16)
                sp.dma_start(bias_row[:], score_bias.partition_broadcast(P)).then_inc(router_in, 16)

                def load(e, i):
                    sp.dma_start(gu_raw[i][:], gate_up_t[e].rearrange("(c p) n -> p c n", p=P)
                                 ).then_inc(gu_in[i], 16)
                    sp.dma_start(dn_raw[i][:], down_t[e]).then_inc(gu_in[i], 16)

                for i in range(2):
                    load(i, i)
                with sp.Fori(0, TURNS - 1) as turn:
                    for i in range(2):
                        sp.wait_ge(w_ready, turn * 2 + (i + 1))
                        load(turn * 2 + (i + 2), i)
                sp.wait_ge(y_added, 2 + TURNS * PER_TURN)
                out_v = out.rearrange("b (t p) d -> p (b t) d", p=P)
                for g in range(B):
                    sp.dma_start(out_v[:, TT * g:TT * g + TT, :], acc[:, TT * g:TT * g + TT, :]
                                 ).then_inc(out_done, 16)
                sp.wait_ge(out_done, 16 * B)

            @block.gpsimd
            def _(pool):
                pool.memset(ident[:], 0.0).then_inc(zeroed, 1)
                pool.wait_ge(zeroed, 1)
                pool.affine_select(out=ident[:], in_=ident[:], compare_op=ALU.not_equal, fill=1.0,
                                   base=0, pattern=[[-1, P]], channel_multiplier=1
                                   ).then_inc(ident_ready, 1)

                def low(done, i):
                    pool.wait_ge(w_hi_ready, done + 1)
                    pool.tensor_tensor(gu_lo[i][:], gu_raw[i][:], gu_hi[i][:].bitcast(F32), ALU.subtract)
                    pool.tensor_tensor(dn_lo[i][:], dn_raw[i][:], dn_hi[i][:].bitcast(F32), ALU.subtract
                                       ).then_inc(w_ready, 1)

                low(0, 0)
                with pool.Fori(0, TURNS - 1) as turn:
                    low(turn * 2 + 1, 1)
                    low(turn * 2 + 2, 0)
                low(E_ROUTED - 1, 1)

            @block.tensor
            def _(pe):
                pe.wait_ge(ident_ready, 1)
                pe.wait_ge(xn_ready, 1)
                for n in range(KD * B):
                    c, g = n % KD, n // KD
                    for t in range(TT):
                        last = pe.transpose(banks[:, n, t * P:(t + 1) * P],
                                            xn[:, TT * g + t, c * P:(c + 1) * P], ident[:])
                    last.then_inc(xt_psum, 1)
                pe.wait_ge(xt_lo_ready, KD * B)
                pe.wait_ge(cls_ready, 2)
                for t in range(TILES):
                    tok = slice(t * P, (t + 1) * P)
                    n = 0
                    for c in range(KD):
                        for u in (xt_hi, xt_lo):
                            for w in (cls_hi, cls_lo):
                                last = pe.matmul(banks[:, t // 8, (t % 8) * E_ALL:(t % 8 + 1) * E_ALL],
                                                 u[:, c, tok], w[:, c, :], start=(n == 0),
                                                 stop=(n == 4 * KD - 1))
                                n += 1
                last.then_inc(logits_psum, 1)
                pe.wait_ge(shifted, 1)

                def front(turn, j):
                    i, chunk = j // CHUNKS % 2, j % CHUNKS
                    if chunk == 0:
                        pe.wait_ge(w_ready, turn * 2 + (j // CHUNKS + 1))
                    if j > 0:
                        pe.wait_ge(h_ready, turn * PER_TURN + j)
                    tok = slice(chunk * 512, (chunk + 1) * 512)
                    for half in range(2):
                        cols = slice(half * INTER, (half + 1) * INTER)
                        n = 0
                        for c in range(KD):
                            for w, u in ((gu_hi, xt_hi), (gu_hi, xt_lo), (gu_lo, xt_hi)):
                                last = pe.matmul(banks[:, 2 * (j % 2) + half, :], w[i][:, c, cols],
                                                 u[:, c, tok], start=(n == 0), stop=(n == 3 * KD - 1))
                                n += 1
                    last.then_inc(gu_psum, 1)

                def back(turn, j):
                    i = j // CHUNKS
                    pe.wait_ge(h_lo_ready, turn * PER_TURN + (j + 1))
                    pe.wait_ge(y_added, turn * PER_TURN + (j + 1))
                    for t in range(4):
                        at = (t % 2) * D
                        for n, (u, w) in enumerate(((h_hi, dn_hi), (h_hi, dn_lo), (h_lo, dn_hi))):
                            last = pe.matmul(banks[:, 4 + 2 * (j % 2) + t // 2, at:at + D],
                                             u[j % 2][:, t * P:(t + 1) * P], w[i][:],
                                             start=(n == 0), stop=(n == 2))
                    last.then_inc(y_psum, 1)

                front(0, 0)
                with pe.Fori(0, TURNS - 1) as turn:
                    for j in range(PER_TURN):
                        front(turn, j + 1)
                        back(turn, j)
                for j in range(PER_TURN):
                    if j + 1 < PER_TURN:
                        front(TURNS - 1, j + 1)
                    back(TURNS - 1, j)

            @block.scalar
            def _(act):
                act.wait_ge(router_in, 32)
                act.activation(cls_hi[:], cls[:], ACT.Copy).then_inc(cls_ready, 1)
                for n in range(KD * B):
                    c, g = n % KD, n // KD
                    act.wait_ge(xt_psum, n + 1)
                    act.activation(xt_hi[:, c, g * T:(g + 1) * T], banks[:, n, :], ACT.Copy
                                   ).then_inc(xt_hi_ready, 1)
                act.wait_ge(shifted, 1)
                act.activation(scores[:], scores[:], ACT.Exp).then_inc(exp_ready, 1)

                def front(turn, j):
                    act.wait_ge(gu_psum, turn * PER_TURN + (j + 1))
                    act.activation(silu[j % 2][:], banks[:, 2 * (j % 2), :], ACT.Silu
                                   ).then_inc(silu_ready, 1)
                    act.wait_ge(h_ready, turn * PER_TURN + (j + 2))
                    act.activation(h_hi[j % 2][:], hidden[j % 2][:], ACT.Copy).then_inc(h_hi_ready, 1)

                def cut(turn, i):
                    act.wait_ge(gu_in[i], turn * 32 + 32)
                    act.activation(gu_hi[i][:], gu_raw[i][:], ACT.Copy)
                    act.activation(dn_hi[i][:], dn_raw[i][:], ACT.Copy).then_inc(w_hi_ready, 1)

                def step(turn, j, last=False):
                    if not (last and j == PER_TURN - 1):
                        front(turn, j + 1)
                    if j == 1:
                        act.wait_ge(y_psum, turn * PER_TURN + 1)
                        cut(turn, 1)
                    if j == CHUNKS + 1 and not last:
                        act.wait_ge(y_psum, turn * PER_TURN + CHUNKS)
                        cut(turn + 1, 0)

                cut(0, 0)
                front(0, 0)
                with act.Fori(0, TURNS - 1) as turn:
                    for j in range(PER_TURN):
                        step(turn, j)
                for j in range(PER_TURN):
                    step(TURNS - 1, j, last=True)

            @block.vector
            def _(dve):
                chain = Chain(dve, dve_chain)
                dve.memset(choice[:, :, E_ALL:], HUGE).then_inc(h_ready, 1)
                dve.wait_ge(x_in, 16 * B)
                layernorm(dve, chain, xn, acc, TILES, stats, mean_var, var[:], rstd[:], tmp[:]
                          ).then_inc(xn_ready, 1)
                dve.wait_ge(cls_ready, 1)
                dve.tensor_tensor(cls_lo[:], cls[:], cls_hi[:].bitcast(F32), ALU.subtract
                                  ).then_inc(cls_ready, 1)
                for n in range(KD * B):
                    c, g = n % KD, n // KD
                    dve.wait_ge(xt_hi_ready, n + 1)
                    dve.tensor_tensor(xt_lo[:, c, g * T:(g + 1) * T], banks[:, n, :],
                                      xt_hi[:, c, g * T:(g + 1) * T].bitcast(F32), ALU.subtract
                                      ).then_inc(xt_lo_ready, 1)
                dve.wait_ge(logits_psum, 1)
                logits = banks[:, 0:2, 0:8 * E_ALL].rearrange("p b (t e) -> p b t e", e=E_ALL)
                grouped = scores[:].rearrange("p (b t) e -> p b t e", b=2)
                for half in range(2):
                    last = dve.tensor_reduce(tmp[:, 8 * half:8 * half + 8], logits[:, half], AX.X, ALU.max)
                chain.then_wait(last)
                for half in range(2):
                    last = dve.tensor_tensor(grouped[:, half], logits[:, half],
                                             tmp[:, 8 * half:8 * half + 8].unsqueeze(2)
                                             .to_broadcast([P, 8, E_ALL]), ALU.subtract)
                last.then_inc(shifted, 1)
                dve.wait_ge(exp_ready, 1)
                chain.then_wait(dve.tensor_reduce(var[:], scores[:], AX.X, ALU.add))
                chain.then_wait(dve.reciprocal(rstd[:], var[:]))
                chain.then_wait(dve.tensor_tensor(scores[:], scores[:],
                                                  rstd[:].unsqueeze(2).to_broadcast([P, TILES, E_ALL]),
                                                  ALU.mult))
                chain.then_wait(dve.tensor_tensor(choice[:, :, 0:E_ALL], scores[:],
                                                  bias_row[:].unsqueeze(1)
                                                  .to_broadcast([P, TILES, E_ALL]), ALU.add))
                for t in range(TILES):
                    last = dve.max(top[:, t, :], choice[:, t, :])
                chain.then_wait(last)
                for t in range(TILES):
                    last = dve.match_replace(left[:, t, :], top[:, t, :], choice[:, t, :], -HUGE)
                chain.then_wait(last)
                chain.then_wait(dve.tensor_tensor(left[:, :, 0:E_ALL], left[:, :, 0:E_ALL],
                                                  choice[:, :, 0:E_ALL], ALU.not_equal))
                chain.then_wait(dve.scalar_tensor_tensor(
                    out=weights[:].rearrange("p e t -> p t e"), in0=left[:, :, 0:E_ALL],
                    scalar=ROUTE_SCALE, in1=scores[:], op0=ALU.mult, op1=ALU.mult))
                chain.then_wait(dve.tensor_reduce(
                    zero_w[:], weights[:, E_ROUTED:, :].rearrange("p e t -> p t e"), AX.X, ALU.add))
                for t in range(TILES):
                    last = dve.scalar_tensor_tensor(out=acc[:, t, :], in0=xn[:, t, :],
                                                    scalar=zero_w[:, t:t + 1], in1=acc[:, t, :],
                                                    op0=ALU.mult, op1=ALU.add)
                last.then_inc(y_added, 2)

                def front(turn, j):
                    if j % CHUNKS == 0:
                        i = j // CHUNKS % 2
                        dve.tensor_copy(current[i][:], weights[:, turn * 2 + j // CHUNKS, :]
                                        ).then_inc(current_ready, 1)
                    dve.wait_ge(silu_ready, turn * PER_TURN + (j + 1))
                    dve.tensor_tensor(hidden[j % 2][:], banks[:, 2 * (j % 2) + 1, :], silu[j % 2][:],
                                      ALU.mult).then_inc(h_ready, 1)
                    dve.wait_ge(h_hi_ready, turn * PER_TURN + (j + 1))
                    dve.tensor_tensor(h_lo[j % 2][:], hidden[j % 2][:], h_hi[j % 2][:].bitcast(F32),
                                      ALU.subtract).then_inc(h_lo_ready, 1)

                def back(turn, j):
                    i, chunk = j // CHUNKS, j % CHUNKS
                    dve.wait_ge(current_ready, turn * 2 + (i + 1))
                    dve.wait_ge(y_added, turn * PER_TURN + (j + 2))
                    dve.wait_ge(y_psum, turn * PER_TURN + (j + 1))
                    for t in range(4):
                        tile = chunk * 4 + t
                        last = dve.scalar_tensor_tensor(
                            out=acc[:, tile, :], in0=banks[:, 4 + 2 * (j % 2) + t // 2,
                                                           (t % 2) * D:(t % 2 + 1) * D],
                            scalar=current[i][:, tile:tile + 1], in1=acc[:, tile, :],
                            op0=ALU.mult, op1=ALU.add)
                    last.then_inc(y_added, 1)

                front(0, 0)
                with dve.Fori(0, TURNS - 1) as turn:
                    for j in range(PER_TURN):
                        front(turn, j + 1)
                        back(turn, j)
                for j in range(PER_TURN):
                    if j + 1 < PER_TURN:
                        front(TURNS - 1, j + 1)
                    back(TURNS - 1, j)


def decoder_layer(nc, x, ctx_t, wq, wk, wv, wo, bo, rel_bias, xwq_t, xbq, xwkv_t, xbkv, q_gamma,
                  k_gamma, cls_t, score_bias, gate_up_t, down_t, out):
    ext_scratch = nc.dram_tensor("extended_bias", (H, P, T + P), F32).ap()
    x1 = nc.dram_tensor("x1", (B, T, D), F32).ap()
    x2 = nc.dram_tensor("x2", (B, T, D), F32).ap()
    self_attention(nc, x, wq, wk, wv, wo, bo, rel_bias, ext_scratch, x1)
    cross_attention(nc, x1, ctx_t, xwq_t, xbq, xwkv_t, xbkv, q_gamma, k_gamma, x2)
    experts(nc, x2, cls_t, score_bias, gate_up_t, down_t, out)


def kernel(**inputs):
    import numpy as np
    import concourse.bacc as bacc
    from concourse.bass_utils import run_bass_kernel_spmd

    given = {k: np.asarray(v) for k, v in inputs.items()}
    wkv = given["L0_xattn_Wkv"].reshape(D, 2, D).transpose(2, 1, 0).reshape(D, 2 * D)
    bkv = given["L0_xattn_bkv"].reshape(D, 2).transpose(1, 0).reshape(2 * D)
    arrays = {
        "x": given["x"],
        "ctx_t": given["ctx_1024"].transpose(0, 2, 1),
        "wq": given["L0_attn_Wq"],
        "wk": given["L0_attn_Wk"],
        "wv": given["L0_attn_Wv"],
        "wo": given["L0_attn_Wo"],
        "bo": given["L0_attn_bo"],
        "rel_bias": given["L0_attn_rel_pos_bias"],
        "xwq_t": given["L0_xattn_Wq"].transpose(1, 0),
        "xbq": given["L0_xattn_bq"],
        "xwkv_t": wkv,
        "xbkv": bkv,
        "q_gamma": given["L0_xattn_q_gamma"],
        "k_gamma": given["L0_xattn_k_gamma"],
        "cls_t": given["L0_ffn_classifier_weight"].transpose(1, 0),
        "score_bias": given["L0_ffn_e_score_correction_bias"],
        "gate_up_t": given["L0_ffn_gate_up_proj"].transpose(0, 2, 1),
        "down_t": given["L0_ffn_down_proj"].transpose(0, 2, 1),
    }
    arrays = {f"in_{k}": np.ascontiguousarray(v) for k, v in arrays.items()}
    nc = bacc.Bacc("TRN2", target_bir_lowering=False, num_devices=1)
    args = [nc.dram_tensor(k, v.shape, mybir.dt.from_np(v.dtype), kind="ExternalInput").ap()
            for k, v in arrays.items()]
    out = nc.dram_tensor("out", (B, T, D), F32, kind="ExternalOutput").ap()
    decoder_layer(nc, *args, out)
    r = run_bass_kernel_spmd(nc, [arrays], core_ids=[0])
    return r.results[0]["out"]
```

```python
from contextlib import ExitStack

import concourse.bass as bass
from concourse import mybir

F32 = mybir.dt.float32
F32R = mybir.dt.float32r
I32 = mybir.dt.int32
ALU = mybir.AluOpType
ACT = mybir.ActivationFunctionType
AX = mybir.AxisListType

P = 128
B, T, D = 4, 512, 256
KD = D // P
TT = T // P
H = 16
DH = 64
PAIRS = H // 2
HD = H * DH
BIAS_LEN = 256
MASKED = -1.0e30
M_KEYS = 1601
XD = D // H
E_ROUTED, E_ALL, TOP_K, INTER = 32, 40, 6, 128
ROUTE_SCALE = 2.5
TILES = B * TT
LN_EPS = 1e-5
RMS_EPS = 1.1920928955078125e-07
RSQRT_MAGIC = 0x5F3759DF


class Chain:

    def __init__(self, eng, sem):
        self.eng, self.sem, self.n = eng, sem, 0

    def then_wait(self, ins):
        self.n += 1
        ins.then_inc(self.sem, 1)
        self.eng.wait_ge(self.sem, self.n)


def rsqrt(dve, chain, out, x, tmp, done=None):
    chain.then_wait(dve.tensor_scalar(out.bitcast(I32), x.bitcast(I32), -0.5, float(RSQRT_MAGIC),
                                      ALU.mult, ALU.add))
    for step in range(3):
        chain.then_wait(dve.scalar_tensor_tensor(out=tmp, in0=out, scalar=-0.5, in1=out,
                                                 op0=ALU.mult, op1=ALU.mult))
        chain.then_wait(dve.tensor_tensor(tmp, tmp, x, ALU.mult))
        last = dve.scalar_tensor_tensor(out=out, in0=tmp, scalar=1.5, in1=out,
                                        op0=ALU.add, op1=ALU.mult)
        if step == 2 and done is not None:
            last.then_inc(done, 1)
        else:
            chain.then_wait(last)


def layernorm(dve, chain, out, x, tiles, stats, mean_var, var, rstd, tmp, done=None):
    for t in range(tiles):
        last = dve.bn_stats(stats[:, t, :], x[:, t, :])
    chain.then_wait(last)
    for t in range(tiles):
        last = dve.bn_aggr(mean_var[:, t, :], stats[:, t, :])
    chain.then_wait(last)
    chain.then_wait(dve.tensor_scalar(var, mean_var[:, 0:tiles, 1], LN_EPS, None, ALU.add))
    rsqrt(dve, chain, rstd, var, tmp)
    for t in range(tiles):
        last = dve.tensor_scalar(out[:, t, :], x[:, t, :], mean_var[:, t, 0:1], rstd[:, t:t + 1],
                                 ALU.subtract, ALU.mult)
        if done is not None and t % TT == TT - 1:
            last.then_inc(done, 1)
    return last


def self_attention(nc, x, wq, wk, wv, wo, bo, bias_rev, ext_scratch, x1):
    STEPS = H * TT
    PER_PAIR = 2 * TT
    TOEP_HEADS = 2
    LAG_T = 3
    LAG_PV = LAG_T + 2
    LAG_OT = LAG_PV + TT - 1
    RECIP_AT = 3
    BIAS_W = T + P
    PT_K = (TT - 1) * P
    PT_W = (TT - 1) * (PT_K + P) + P

    with ExitStack() as ctx:
        def sb(name, shape, dt=F32):
            return ctx.enter_context(nc.sbuf_tensor("sa_" + name, shape, dt))

        def bank(name):
            return ctx.enter_context(nc.psum_tensor("sa_" + name, [P, 512], F32))

        sems = []

        def sem(name):
            sems.append(ctx.enter_context(nc.semaphore("sa_" + name)))
            return sems[-1]

        ident = sb("ident", [P, P])
        w_hi = [sb(f"w{n}_hi", [P, KD, HD], F32R) for n in "qkv"]
        w_lo = [sb(f"w{n}_lo", [P, KD, HD], F32R) for n in "qkv"]
        wo_sb = sb("wo", [P, PAIRS, D])
        bo_row = sb("bo", [P, D])
        toeplitz = sb("toeplitz", [P, H, T])
        x_sb = sb("x", [P, TT, D])
        xn = sb("xn", [P, TT, D])
        xt_hi = sb("xt_hi", [P, KD, T], F32R)
        xt_lo = sb("xt_lo", [P, KD, T], F32R)
        v_sb = sb("v", [P, TT, HD])
        q_hi = [[sb(f"q_hi{i}{a}", [P, T], F32R) for a in range(2)] for i in range(2)]
        q_lo = [[sb(f"q_lo{i}{a}", [P, T], F32R) for a in range(2)] for i in range(2)]
        k_hi = [sb(f"k_hi{i}", [P, T], F32R) for i in range(2)]
        k_lo = [sb(f"k_lo{i}", [P, T], F32R) for i in range(2)]
        probs = sb("probs", [P, 4, T])
        pt = sb("pt", [P, 4 * PT_W + TT * P])
        ot = sb("ot", [P, PAIRS, T])
        recip_wide = sb("recip_wide", [P, TT, P])
        recip_bc = sb("recip_bc", [P, T])
        stats = sb("stats", [P, TT, 6])
        mean_var = sb("mean_var", [P, TT, 2])
        var = sb("var", [P, TT])
        rstd = sb("rstd", [P, TT])
        tmp = sb("tmp", [P, TT])
        neg_max = sb("neg_max", [P, STEPS])
        sums = sb("sums", [P, STEPS])
        recip = sb("recip", [P, STEPS])

        pj = [bank(f"pj{i}") for i in range(2)]
        ps = [bank(f"ps{i}") for i in range(2)]
        ptr = [bank(f"ptr{i}") for i in range(2)]
        po = bank("po")
        pr = bank("pr")

        toep_in = sem("toep_in")
        wo_in = sem("wo_in")
        x1_out = sem("x1_out")

        once = len(sems)
        x0_in = sem("x0_in")
        w_in = sem("w_in")
        bias_in = sem("bias_in")
        ext_out = sem("ext_out")
        w_hi_done = sem("w_hi_done")
        ext_done = sem("ext_done")
        zeroed = sem("zeroed")
        ident_ready = sem("ident_ready")
        xn0_ready = sem("xn0_ready")
        xt0_psum = sem("xt0_psum")
        xt0_hi_ready = sem("xt0_hi_ready")
        set_chain = sem("set_chain")
        ext = x_sb[:].rearrange("p t d -> p (t d)")[0:H, 0:BIAS_W]
        raw = [ot[:, 0:4, :], ot[:, 4:8, :], v_sb[:, 0:2, :]]
        raw = [r.rearrange("p a b -> p (a b)") for r in raw]

        with nc.Block() as block:
            @block.sync
            def _(sp):
                sp.dma_start(xn[:], x[0].rearrange("(t p) d -> p t d", p=P)).then_inc(x0_in, 16)
                sp.dma_start(ext[:, P:P + BIAS_LEN], bias_rev).then_inc(bias_in, 16)
                for r, w in zip(raw, (wq, wk, wv)):
                    sp.dma_start(r.rearrange("p (c n) -> p c n", c=KD),
                                 w.rearrange("(c p) n -> p c n", p=P)).then_inc(w_in, 16)
                sp.wait_ge(ext_done, 2)
                sp.dma_start(ext_scratch, ext).then_inc(ext_out, 16)
                sp.dma_start(wo_sb[:], wo.rearrange("(c p) n -> p c n", p=P)).then_inc(wo_in, 16)
                sp.dma_start(bo_row[:], bo.partition_broadcast(P)).then_inc(x1_out, 16)
                sp.wait_ge(ext_out, 16)
                for h in range(0, H, TOEP_HEADS):
                    sp.dma_start(toeplitz[:, h:h + TOEP_HEADS, :],
                                 bass.AP(ext_scratch.tensor, h * BIAS_W + 1,
                                         [[1, P], [BIAS_W, TOEP_HEADS], [1, T]])).then_inc(toep_in, 16)

            @block.gpsimd
            def _(pool):
                pool.memset(ident[:], 0.0).then_inc(zeroed, 1)
                pool.wait_ge(zeroed, 1)
                pool.affine_select(out=ident[:], in_=ident[:], compare_op=ALU.not_equal, fill=1.0,
                                   base=0, pattern=[[-1, P]], channel_multiplier=1
                                   ).then_inc(ident_ready, 1)

            @block.tensor
            def _(pe):
                pe.wait_ge(ident_ready, 1)
                pe.wait_ge(xn0_ready, 1)
                for c in range(KD):
                    for t in range(TT):
                        last = pe.transpose(ptr[c][:, t * P:(t + 1) * P],
                                            xn[:, t, c * P:(c + 1) * P], ident[:])
                    last.then_inc(xt0_psum, 1)

            @block.scalar
            def _(act):
                for c in range(KD):
                    act.wait_ge(xt0_psum, c + 1)
                    act.activation(xt_hi[:, c, :], ptr[c][:], ACT.Copy).then_inc(xt0_hi_ready, 1)
                act.wait_ge(w_in, 48)
                for r, hi in zip(raw, w_hi):
                    act.activation(hi[:].rearrange("p c n -> p (c n)"), r, ACT.Copy
                                   ).then_inc(w_hi_done, 1)

            @block.vector
            def _(dve):
                chain = Chain(dve, set_chain)
                dve.memset(ext[:, 0:P], MASKED).then_inc(ext_done, 1)
                dve.wait_ge(bias_in, 16)
                dve.tensor_copy(ext[:, P + BIAS_LEN:],
                                ext[:, P + BIAS_LEN - 1:P + BIAS_LEN].to_broadcast([H, BIAS_LEN])
                                ).then_inc(ext_done, 1)
                for i in range(2):
                    for a in range(2):
                        other = slice(DH * (1 - a), DH * (2 - a))
                        dve.memset(q_hi[i][a][other, :].bitcast(F32), 0.0)
                        dve.memset(q_lo[i][a][other, :].bitcast(F32), 0.0)
                dve.wait_ge(x0_in, 16)
                layernorm(dve, chain, xn, xn, TT, stats, mean_var, var[:], rstd[:], tmp[:]
                          ).then_inc(xn0_ready, 1)
                for c in range(KD):
                    dve.wait_ge(xt0_hi_ready, c + 1)
                    dve.tensor_tensor(xt_lo[:, c, :], ptr[c][:], xt_hi[:, c, :].bitcast(F32),
                                      ALU.subtract)
                for n, (r, hi, lo) in enumerate(zip(raw, w_hi, w_lo)):
                    dve.wait_ge(w_hi_done, n + 1)
                    dve.tensor_tensor(lo[:].rearrange("p c n -> p (c n)"), r,
                                      hi[:].rearrange("p c n -> p (c n)").bitcast(F32),
                                      ALU.subtract)
        nc.all_engine_barrier(sems_to_clear=range(sems[once].num, sems[-1].num + 1))

        first = len(sems)
        x_next_in = sem("x_next_in")
        x_in = sem("x_in")
        xn_ready = sem("xn_ready")
        xt_psum = sem("xt_psum")
        xt_hi_ready = sem("xt_hi_ready")
        v_psum = sem("v_psum")
        v_even = sem("v_even")
        v_odd = sem("v_odd")
        qk_psum = sem("qk_psum")
        qk_hi_ready = sem("qk_hi_ready")
        qk_lo_ready = sem("qk_lo_ready")
        s_psum = sem("s_psum")
        logits_ready = sem("logits_ready")
        probs_ready = sem("probs_ready")
        pt_psum = sem("pt_psum")
        pt_even = sem("pt_even")
        pt_odd = sem("pt_odd")
        recip_ready = sem("recip_ready")
        recip_wide_ready = sem("recip_wide_ready")
        r_psum = sem("r_psum")
        r_ready = sem("r_ready")
        o_psum = sem("o_psum")
        ot_ready = sem("ot_ready")
        y_psum = sem("y_psum")
        x_bo_ready = sem("x_bo_ready")
        x1_ready = sem("x1_ready")
        dve_chain = sem("dve_chain")
        y_banks = pj + ps

        def tile_of(t):
            h, r = divmod(t, TT)
            return h, r, (r + 1) * P

        def pt_at(h, k, r):
            return (h % 4) * PT_W + k * PT_K + r * P

        def pt_blocks(h, r):
            at = pt_at(h, 0, r)
            return pt[:, at:at + (r + 1) * PT_K].rearrange("p (k c) -> p k c", c=PT_K)[:, :, 0:P]

        def turned(t):
            h, r, w = tile_of(t)
            return ptr[t % 2][:, 0:w].rearrange("p (k c) -> p k c", c=P)

        with nc.Fori(0, B) as b:
            with nc.Block() as block:
                @block.sync
                def _(sp):
                    sp.dma_start(xn[:], x[(b + 1) % B].rearrange("(t p) d -> p t d", p=P)
                                 ).then_inc(x_next_in, 16)
                    sp.wait_ge(x1_out, b * 16 + 16)
                    sp.dma_start(x_sb[:], x[b].rearrange("(t p) d -> p t d", p=P)).then_inc(x_in, 16)
                    sp.wait_ge(x1_ready, TT)
                    sp.dma_start(x1[b].rearrange("(t p) d -> p t d", p=P), x_sb[:]).then_inc(x1_out, 16)

                @block.gpsimd
                def _(pool):
                    pool.wait_ge(x_in, 16)
                    for t in range(TT):
                        last = pool.tensor_tensor(x_sb[:, t, :], x_sb[:, t, :], bo_row[:], ALU.add)
                    last.then_inc(x_bo_ready, 1)
                    for p in range(PAIRS):
                        pool.wait_ge(recip_ready, p + 1)
                        if p >= 1:
                            pool.wait_ge(r_psum, p)
                        cols = recip[:, p * PER_PAIR:(p + 1) * PER_PAIR]
                        pool.tensor_copy(recip_wide[:, :, :].rearrange("p r (a d) -> p r a d", a=2),
                                         cols.rearrange("p (a r) -> p r a", a=2).unsqueeze(3)
                                         .to_broadcast([P, TT, 2, DH])).then_inc(recip_wide_ready, 1)

                @block.tensor
                def _(pe):
                    def product(out, parts, chunks):
                        n = 0
                        for c in range(chunks):
                            (a_hi, a_lo), (b_hi, b_lo) = parts(c)
                            for u, v in ((a_hi, b_hi), (a_hi, b_lo), (a_lo, b_hi)):
                                last = pe.matmul(out, u, v, start=(n == 0), stop=(n == 3 * chunks - 1))
                                n += 1
                        return last

                    def project(p, which):
                        if p >= 1:
                            pe.wait_ge(qk_lo_ready, 2 * (p - 1) + which + 1)
                        cols = slice(p * P, (p + 1) * P)
                        product(pj[which][:],
                                lambda c: ((w_hi[which][:, c, cols], w_lo[which][:, c, cols]),
                                           (xt_hi[:, c, :], xt_lo[:, c, :])), KD
                                ).then_inc(qk_psum, 1)

                    def scores(t):
                        h, r, w = tile_of(t)
                        p, a = divmod(h, 2)
                        if t % PER_PAIR == 0:
                            pe.wait_ge(qk_lo_ready, 2 * (p + 1))
                        if t >= 2:
                            pe.wait_ge(logits_ready, t - 1)
                        q = slice(r * P, (r + 1) * P)
                        product(ps[t % 2][:, 0:w],
                                lambda c: ((q_hi[p % 2][a][:, q], q_lo[p % 2][a][:, q]),
                                           (k_hi[p % 2][:, 0:w], k_lo[p % 2][:, 0:w])), 1
                                ).then_inc(s_psum, 1)

                    def turn(t):
                        h, r, w = tile_of(t)
                        pe.wait_ge(probs_ready, t + 1)
                        if t >= 2:
                            pe.wait_ge((pt_even, pt_odd)[t % 2], t // 2)
                        else:
                            pe.wait_ge((v_even, v_odd)[t], TT)
                        for k in range(r + 1):
                            last = pe.transpose(ptr[t % 2][:, k * P:(k + 1) * P],
                                                probs[:, t % 4, k * P:(k + 1) * P], ident[:])
                        last.then_inc(pt_psum, 1)

                    def times_v(p, k):
                        if k == 0:
                            pe.wait_ge(pt_even, TT * (p + 1))
                            pe.wait_ge(pt_odd, TT * (p + 1))
                            if p >= 1:
                                pe.wait_ge(ot_ready, p)
                        for a in range(2):
                            h = 2 * p + a
                            last = pe.matmul(po[a * DH:(a + 1) * DH, k * P:T],
                                             v_sb[:, k, h * DH:(h + 1) * DH],
                                             pt[:, pt_at(h, k, k):pt_at(h, k, TT)],
                                             start=(k == 0), stop=(k == TT - 1))
                        if k == TT - 1:
                            last.then_inc(o_psum, 1)

                    def turn_recip(p):
                        pe.wait_ge(recip_wide_ready, p + 1)
                        for r in range(TT):
                            last = pe.transpose(pr[:, r * P:(r + 1) * P], recip_wide[:, r, :], ident[:])
                        last.then_inc(r_psum, 1)

                    def turn_next():
                        pe.wait_ge(xn_ready, 1)
                        for c in range(KD):
                            for t in range(TT):
                                last = pe.transpose(ptr[c][:, t * P:(t + 1) * P],
                                                    xn[:, t, c * P:(c + 1) * P], ident[:])
                            last.then_inc(xt_psum, 1)

                    project(0, 0)
                    project(0, 1)
                    for u in range(2 * TT):
                        t, half = divmod(u, 2)
                        if u == 2:
                            pe.wait_ge(v_even, 1)
                        elif u == 3:
                            pe.wait_ge(v_odd, 1)
                        elif u > 3:
                            pe.wait_ge((v_even, v_odd)[u % 2], u // 2)
                        tok, cols = slice(t * P, (t + 1) * P), slice(half * 512, (half + 1) * 512)
                        product(ptr[u % 2][:],
                                lambda c: ((xt_hi[:, c, tok], xt_lo[:, c, tok]),
                                           (w_hi[2][:, c, cols], w_lo[2][:, c, cols])), KD
                                ).then_inc(v_psum, 1)
                    for s in range(STEPS + PER_PAIR):
                        if s < STEPS:
                            scores(s)
                        if s % PER_PAIR in (2, 4) and s // PER_PAIR + 1 < PAIRS:
                            project(s // PER_PAIR + 1, s % PER_PAIR // 2 - 1)
                        if LAG_T <= s < STEPS + LAG_T:
                            turn(s - LAG_T)
                        first_v = s - LAG_PV - (PER_PAIR - 1)
                        if first_v >= 0 and first_v % PER_PAIR < TT and first_v < STEPS:
                            times_v(first_v // PER_PAIR, first_v % PER_PAIR)
                        if first_v >= 0 and first_v % PER_PAIR == RECIP_AT and first_v < STEPS:
                            turn_recip(first_v // PER_PAIR)
                    pe.wait_ge(ot_ready, PAIRS)
                    pe.wait_ge(wo_in, 16)
                    for t in range(TT):
                        if t == TT - 1:
                            turn_next()
                        for p in range(PAIRS):
                            last = pe.matmul(y_banks[t][:, 0:D], ot[:, p, t * P:(t + 1) * P],
                                             wo_sb[:, p, :], start=(p == 0), stop=(p == PAIRS - 1))
                        last.then_inc(y_psum, 1)

                @block.scalar
                def _(act):
                    def part_q(p):
                        act.wait_ge(qk_psum, 2 * p + 1)
                        if p >= 2:
                            act.wait_ge(s_psum, PER_PAIR * (p - 1))
                        for a in range(2):
                            rows = slice(a * DH, (a + 1) * DH)
                            last = act.activation(q_hi[p % 2][a][rows, :], pj[0][rows, :], ACT.Copy)
                        last.then_inc(qk_hi_ready, 1)

                    def part_k(p):
                        act.wait_ge(qk_psum, 2 * p + 2)
                        act.activation(k_hi[p % 2][:], pj[1][:], ACT.Copy).then_inc(qk_hi_ready, 1)

                    def exps(t):
                        h, r, w = tile_of(t)
                        act.wait_ge(logits_ready, t + 1)
                        act.activation(probs[:, t % 4, 0:w], probs[:, t % 4, 0:w], ACT.Exp,
                                       bias=neg_max[:, t:t + 1], scale=-1.0,
                                       accum_out=sums[:, t:t + 1]).then_inc(probs_ready, 1)

                    part_q(0)
                    part_k(0)
                    for u in range(1, 2 * TT, 2):
                        act.wait_ge(v_psum, u + 1)
                        act.activation(v_sb[:, u // 2, 512:1024], ptr[1][:], ACT.Copy
                                       ).then_inc(v_odd, 1)
                    for s in range(STEPS + PER_PAIR):
                        if s < STEPS:
                            exps(s)
                        if s % PER_PAIR == 2 and s // PER_PAIR + 1 < PAIRS:
                            part_q(s // PER_PAIR + 1)
                        if s % PER_PAIR == 4 and s // PER_PAIR + 1 < PAIRS:
                            part_k(s // PER_PAIR + 1)
                        t = s - LAG_T
                        if 0 <= t < STEPS and t % 2 == 1:
                            h, r, w = tile_of(t)
                            act.wait_ge(pt_psum, t + 1)
                            if h >= 4:
                                act.wait_ge(o_psum, (h - 4) // 2 + 1)
                            act.activation(pt_blocks(h, r), turned(t), ACT.Copy).then_inc(pt_odd, 1)
                        if (s - LAG_OT) % PER_PAIR == PER_PAIR - 1 and s >= LAG_OT:
                            p = (s - LAG_OT) // PER_PAIR
                            act.wait_ge(r_psum, p + 1)
                            if p >= 1:
                                act.wait_ge(ot_ready, p)
                            act.activation(recip_bc[:], pr[:], ACT.Copy).then_inc(r_ready, 1)
                    for c in range(KD):
                        act.wait_ge(xt_psum, c + 1)
                        act.activation(xt_hi[:, c, :], ptr[c][:], ACT.Copy).then_inc(xt_hi_ready, 1)

                @block.vector
                def _(dve):
                    chain = Chain(dve, dve_chain)
                    def low_q(p):
                        dve.wait_ge(qk_hi_ready, 2 * p + 1)
                        for a in range(2):
                            rows = slice(a * DH, (a + 1) * DH)
                            last = dve.tensor_tensor(q_lo[p % 2][a][rows, :], pj[0][rows, :],
                                                     q_hi[p % 2][a][rows, :].bitcast(F32), ALU.subtract)
                        last.then_inc(qk_lo_ready, 1)

                    def low_k(p):
                        dve.wait_ge(qk_hi_ready, 2 * p + 2)
                        dve.tensor_tensor(k_lo[p % 2][:], pj[1][:], k_hi[p % 2][:].bitcast(F32),
                                          ALU.subtract).then_inc(qk_lo_ready, 1)

                    def biased(t):
                        h, r, w = tile_of(t)
                        dve.wait_ge(s_psum, t + 1)
                        if t >= 4:
                            dve.wait_ge(pt_psum, t - 3)
                        dve.tensor_tensor_reduce(out=probs[:, t % 4, 0:w], in0=ps[t % 2][:, 0:w],
                                                 in1=toeplitz[:, h, w - 1::-1], scale=-1.0 / DH,
                                                 scalar=3.0e38, op0=ALU.add, op1=ALU.min,
                                                 accum_out=neg_max[:, t:t + 1]
                                                 ).then_inc(logits_ready, 1)

                    low_q(0)
                    low_k(0)
                    for u in range(0, 2 * TT, 2):
                        dve.wait_ge(v_psum, u + 1)
                        dve.tensor_copy(v_sb[:, u // 2, 0:512], ptr[0][:]).then_inc(v_even, 1)
                    dve.wait_ge(toep_in, 16 * H // TOEP_HEADS)
                    for s in range(STEPS + PER_PAIR):
                        if s < STEPS:
                            biased(s)
                        if s % PER_PAIR == 2 and s // PER_PAIR + 1 < PAIRS:
                            low_q(s // PER_PAIR + 1)
                        if s % PER_PAIR == 4 and s // PER_PAIR + 1 < PAIRS:
                            low_k(s // PER_PAIR + 1)
                        t = s - LAG_T
                        if 0 <= t < STEPS and t % 2 == 0:
                            h, r, w = tile_of(t)
                            dve.wait_ge(pt_psum, t + 1)
                            if h >= 4:
                                dve.wait_ge(o_psum, (h - 4) // 2 + 1)
                            dve.tensor_copy(pt_blocks(h, r), turned(t)).then_inc(pt_even, 1)
                        if t % PER_PAIR == PER_PAIR - 1 and 0 <= t < STEPS:
                            p = t // PER_PAIR
                            dve.wait_ge(probs_ready, PER_PAIR * (p + 1))
                            cols = slice(p * PER_PAIR, (p + 1) * PER_PAIR)
                            dve.reciprocal(recip[:, cols], sums[:, cols]).then_inc(recip_ready, 1)
                        if (s - LAG_OT) % PER_PAIR == PER_PAIR - 1 and s >= LAG_OT:
                            p = (s - LAG_OT) // PER_PAIR
                            dve.wait_ge(o_psum, p + 1)
                            dve.wait_ge(r_ready, p + 1)
                            dve.tensor_tensor(ot[:, p, :], po[:], recip_bc[:], ALU.mult
                                              ).then_inc(ot_ready, 1)
                    dve.wait_ge(x_next_in, 16)
                    layernorm(dve, chain, xn, xn, TT, stats, mean_var, var[:], rstd[:], tmp[:]
                              ).then_inc(xn_ready, 1)
                    dve.wait_ge(x_bo_ready, 1)
                    for t in range(TT):
                        if t == TT - 1:
                            for c in range(KD):
                                dve.wait_ge(xt_hi_ready, c + 1)
                                dve.tensor_tensor(xt_lo[:, c, :], ptr[c][:],
                                                  xt_hi[:, c, :].bitcast(F32), ALU.subtract)
                        dve.wait_ge(y_psum, t + 1)
                        dve.tensor_tensor(x_sb[:, t, :], y_banks[t][:, 0:D], x_sb[:, t, :], ALU.add
                                          ).then_inc(x1_ready, 1)
            nc.all_engine_barrier(sems_to_clear=range(sems[first].num, sems[-1].num + 1))
        with nc.Block() as block:
            @block.sync
            def _(sp):
                sp.wait_ge(x1_out, 16 * B + 16)
        nc.all_engine_barrier(sems_to_clear=range(sems[0].num, sems[once - 1].num + 1))


def cross_attention(nc, x1, ctx_t, wq_t, bq, wkv_t, bkv, q_gamma, k_gamma, x2):
    SAFE = 40.0
    SLOT = 4 * XD
    SHIFT = 3 * XD
    QUADS = H // 4
    KT = -(-M_KEYS // P)
    GROUPS = [(0, 4), (4, 8), (8, 12), (12, KT)]
    ENDS = [hi - 1 for lo, hi in GROUPS]
    CUT_AFTER = [hi - 1 for lo, hi in GROUPS[:-2]]
    LAG_K = 7
    UNITS = QUADS * KT * 2
    DEEP = 3
    RING = 6
    LAG = 4
    TURN_X_AT = 0
    PROJECT_Q_AT = 0
    NORM_Q_AT = 0
    HIGH_Q_AT = 3
    LOW_Q_AT = 4
    TURN_Q_AT = 6
    SPAN = 402
    SPAN_AT = [0, 400, 800, M_KEYS - SPAN]

    with ExitStack() as ctx:
        def sb(name, shape, dt=F32):
            return ctx.enter_context(nc.sbuf_tensor("xa_" + name, shape, dt))

        sems = []

        def sem(name):
            sems.append(ctx.enter_context(nc.semaphore("xa_" + name)))
            return sems[-1]

        ident = sb("ident", [P, P])
        wq_sb = sb("wq", [P, KD, D])
        wkv_hi = sb("wkv_hi", [P, KD, 2 * D], F32R)
        wkv_lo = sb("wkv_lo", [P, KD, 2 * D], F32R)
        bq_row = sb("bq", [P, D])
        bkv_row = sb("bkv", [P, 2 * D])
        gammas = sb("gammas", [P, 2, XD])
        gain = sb("gain", [P, XD])
        bound = sb("bound", [P, 1])
        unsafe = sb("unsafe", [P, 1], I32)
        x_sb = sb("x", [P, TT, D])
        xn = sb("xn", [P, TT, D])
        q_tok = sb("q_tok", [P, TT, H, SLOT], F32R)
        q_aug = sb("q_aug", [P, H, T], F32R)
        k_tok = [sb(f"k_tok{i}", [P, H, SLOT], F32R) for i in range(2)]
        k_aug = sb("k_aug", [P, PAIRS, M_KEYS + 1], F32R)
        v_one = sb("v_one", [P, KT, H, XD + 1])
        maxima = sb("maxima", [P, H, TT, 2])
        raw = [sb(f"raw{i}", [P, KD, 4 * P]) for i in range(2)]
        ct_hi = [sb(f"ct_hi{i}", [P, KD, 4 * P], F32R) for i in range(2)]
        ct_lo = [sb(f"ct_lo{i}", [P, KD, 4 * P], F32R) for i in range(2)]
        stats = sb("stats", [P, TT, 6])
        mean_var = sb("mean_var", [P, TT, 2])
        var = sb("var", [P, TT])
        rstd = sb("rstd", [P, TT])
        tmp = sb("tmp", [P, TT])
        square_sum = sb("square_sum", [P, 4 * H])
        rms = sb("rms", [P, 4 * H])
        rms_q = sb("rms_q", [P, 4 * H])
        rms_tmp = sb("rms_tmp", [P, 4 * H])

        outer = ctx
        with ExitStack() as ctx:
            xt = sb("xt", [P, KD, T])
            qb = sb("qb", [P, TT, D])
            kb = [sb(f"kb{i}", [P, 4, D]) for i in range(2)]
            sq = [sb(f"sq{i}", [P, 4, D]) for i in range(2)]
        ctx = outer
        probs = sb("probs", [P, RING, 2, T])
        o_sb = [sb(f"o{i}", [P, T]) for i in range(2)]
        o_norm = sb("o_norm", [P, TT, 4, XD])
        rec = sb("rec", [P, TT, 4])

        banks = ctx.enter_context(nc.psum_tensor("xa_banks", [P, 8, 512], F32))

        x2_out = sem("x2_out")

        wkv_raw = x_sb[:].rearrange("p t d -> p (t d)").rearrange("p (c n) -> p c n", c=KD)
        once = len(sems)
        w_in = sem("w_in")
        x0_in = sem("x0_in")
        ctx0_in = [sem("ctx0_in0"), sem("ctx0_in1")]
        ct0_hi_done = sem("ct0_hi_done")
        wkv_in = sem("wkv_in")
        gain_done = sem("gain_done")
        hi_done = sem("hi_done")
        zeroed = sem("zeroed")
        set_chain = sem("set_chain")

        with nc.Block() as block:
            @block.sync
            def _(sp):
                sp.dma_start(xn[:], x1[0].rearrange("(t p) d -> p t d", p=P)).then_inc(x0_in, 16)
                sp.dma_start(wkv_raw, wkv_t.rearrange("(c p) n -> p c n", p=P)).then_inc(wkv_in, 16)
                for g in range(2):
                    sp.dma_start(raw[g][:], ctx_t[0].rearrange("(c p) m -> p c m", p=P)
                                 [:, :, g * 4 * P:(g + 1) * 4 * P]).then_inc(ctx0_in[g], 16)
                sp.dma_start(wq_sb[:], wq_t.rearrange("(c p) n -> p c n", p=P)).then_inc(w_in, 16)
                sp.dma_start(bq_row[:], bq.partition_broadcast(P)).then_inc(x2_out, 16)
                sp.dma_start(bkv_row[:], bkv.partition_broadcast(P)).then_inc(w_in, 16)
                sp.dma_start(gammas[:, 0, :], q_gamma.partition_broadcast(P)).then_inc(w_in, 16)
                sp.dma_start(gammas[:, 1, :], k_gamma.partition_broadcast(P)).then_inc(w_in, 16)
                sp.wait_ge(x2_out, 16)

            @block.gpsimd
            def _(pool):
                pool.memset(ident[:], 0.0).then_inc(zeroed, 1)
                pool.wait_ge(zeroed, 1)
                pool.affine_select(out=ident[:], in_=ident[:], compare_op=ALU.not_equal, fill=1.0,
                                   base=0, pattern=[[-1, P]], channel_multiplier=1)
                pool.memset(v_one[:, :, :, XD:XD + 1], 1.0).then_inc(zeroed, 1)
                for a in range(2):
                    pool.wait_ge(zeroed, a + 2)
                    rest = q_aug[SLOT * (1 - a):SLOT * (2 - a), a:H:2, :]
                    pool.memset(rest.bitcast(F32), 0.0).then_inc(zeroed, 1)

            @block.scalar
            def _(act):
                act.wait_ge(wkv_in, 16)
                act.activation(wkv_hi[:], wkv_raw, ACT.Copy).then_inc(hi_done, 1)
                for g in range(2):
                    act.wait_ge(ctx0_in[g], 16)
                    act.activation(ct_hi[g][:], raw[g][:], ACT.Copy).then_inc(ct0_hi_done, 1)

            @block.vector
            def _(dve):
                chain = Chain(dve, set_chain)
                for k in k_tok:
                    dve.memset(k[:].bitcast(F32), 0.0)
                last = dve.memset(q_tok[:, :, :, SHIFT:SLOT].bitcast(F32), 0.0)
                chain.then_wait(last)
                for k in k_tok:
                    dve.memset(k[:, :, SHIFT:SHIFT + 1].bitcast(F32), 1.0)
                dve.memset(banks[:, 6, :], 0.0)
                dve.wait_ge(w_in, 64)
                chain.then_wait(dve.tensor_tensor(gain[:], gammas[:, 0, :], gammas[:, 1, :], ALU.mult))
                chain.then_wait(dve.tensor_reduce(bound[:], gain[:], AX.X, ALU.max,
                                                  apply_absolute_value=True))
                chain.then_wait(dve.tensor_scalar(unsafe[:], bound[:], SAFE / 4.0, None, ALU.is_gt))
                dve.tensor_scalar(gain[:], gain[:], float(XD) ** -0.5, None, ALU.mult
                                  ).then_inc(gain_done, 1)
                dve.wait_ge(hi_done, 1)
                dve.tensor_tensor(wkv_lo[:], wkv_raw, wkv_hi[:].bitcast(F32), ALU.subtract)
                dve.wait_ge(x0_in, 16)
                layernorm(dve, chain, xn, xn, TT, stats, mean_var, var[:], rstd[:], tmp[:])
                for g in range(2):
                    dve.wait_ge(ct0_hi_done, g + 1)
                    dve.tensor_tensor(ct_lo[g][:], raw[g][:], ct_hi[g][:].bitcast(F32), ALU.subtract)
        nc.all_engine_barrier(sems_to_clear=range(sems[once].num, sems[-1].num + 1))

        first = len(sems)
        x_in = sem("x_in")
        ctx_in = [sem("ctx_in0"), sem("ctx_in1")]
        next_in = [sem("next_in0"), sem("next_in1")]
        next_hi = sem("next_hi")
        x_next_in = sem("x_next_in")
        xt_psum = sem("xt_psum")
        xt_ready = sem("xt_ready")
        q_psum = sem("q_psum")
        q_biased = sem("q_biased")
        q_hi_ready = sem("q_hi_ready")
        q_tok_ready = sem("q_tok_ready")
        qt_psum = sem("qt_psum")
        q_aug_a = sem("q_aug_a")
        q_aug_b = sem("q_aug_b")
        ct_hi_ready = sem("ct_hi_ready")
        ct_lo_ready = sem("ct_lo_ready")
        kv_psum = sem("kv_psum")
        k_out = sem("k_out")
        kb_ready = sem("kb_ready")
        v_ready = sem("v_ready")
        sq_ready = sem("sq_ready")
        rms_ready = sem("rms_ready")
        kn_ready = sem("kn_ready")
        k_hi_ready = sem("k_hi_ready")
        k_tok_ready = sem("k_tok_ready")
        kt_psum = sem("kt_psum")
        k_aug_a = sem("k_aug_a")
        k_aug_b = sem("k_aug_b")
        max_psum = sem("max_psum")
        max_ready = sem("max_ready")
        shift_ready = sem("shift_ready")
        qt2_psum = sem("qt2_psum")
        q2_aug_a = sem("q2_aug_a")
        q2_aug_b = sem("q2_aug_b")
        s_psum = sem("s_psum")
        probs_ready = sem("probs_ready")
        pv_done = sem("pv_done")
        o_ready = sem("o_ready")
        ot_psum = sem("ot_psum")
        o_norm_ready = sem("o_norm_ready")
        x_bv_ready = sem("x_bv_ready")
        x2_part = sem("x2_part")
        dve_chain = sem("dve_chain")

        def rows_of(c):
            return min(P, M_KEYS - c * P)

        def unit(n):
            g, rest = divmod(n, 2 * KT)
            return g, rest // 2, rest % 2, rows_of(rest // 2)

        with nc.Fori(0, B) as b:
            with nc.Block() as block:
                @block.sync
                def _(sp):
                    def load(batch, g, landed):
                        lo, hi = GROUPS[g]
                        n = min(M_KEYS, hi * P) - lo * P
                        sp.dma_start(raw[g % 2][:, :, 0:n],
                                     ctx_t[batch].rearrange("(c p) m -> p c m", p=P)
                                     [:, :, lo * P:lo * P + n]).then_inc(landed, 16)

                    load(b, 2, ctx_in[0])
                    load(b, 3, ctx_in[1])
                    sp.wait_ge(x2_out, b * 16 + 16)
                    sp.dma_start(x_sb[:], x1[b].rearrange("(t p) d -> p t d", p=P)).then_inc(x_in, 16)
                    sp.wait_ge(q_biased, TT + 1)
                    sp.dma_start(xn[:], x1[(b + 1) % B].rearrange("(t p) d -> p t d", p=P)
                                 ).then_inc(x_next_in, 16)
                    for g in range(2):
                        sp.wait_ge(ct_lo_ready, g + 1)
                        load((b + 1) % B, g, next_in[g])
                    sp.wait_ge(x2_part, QUADS)
                    sp.dma_start(x2[b].rearrange("(t p) d -> p t d", p=P), x_sb[:]).then_inc(x2_out, 16)

                @block.gpsimd
                def _(pool):
                    pool.wait_ge(x_in, 16)
                    pool.tensor_tensor(x_sb[:], x_sb[:],
                                       bkv_row[:, D:2 * D].unsqueeze(1).to_broadcast([P, TT, D]),
                                       ALU.add).then_inc(x_bv_ready, 1)
                    for g, (lo, hi) in enumerate(GROUPS):
                        for c in range(lo, hi):
                            m, i = rows_of(c), c % 4
                            pool.wait_ge(k_out, c + 1)
                            pool.tensor_tensor(kb[g % 2][0:m, i, :], kb[g % 2][0:m, i, :],
                                               bkv_row[0:m, 0:D], ALU.add).then_inc(kb_ready, 1)
                            pool.wait_ge(kb_ready, c + 1)
                            if g >= 2:
                                pool.wait_ge(k_tok_ready, c - 7)
                            pool.tensor_tensor(sq[g % 2][0:m, i, :], kb[g % 2][0:m, i, :], kb[g % 2][0:m, i, :], ALU.mult
                                               ).then_inc(sq_ready, 1)
                        pool.wait_ge(rms_ready, g + 1)
                        for c in range(lo, hi):
                            m, i = rows_of(c), c % 4
                            pool.tensor_tensor(
                                sq[g % 2][0:m, i, :].rearrange("p (h d) -> p h d", h=H),
                                kb[g % 2][0:m, i, :].rearrange("p (h d) -> p h d", h=H),
                                rms[0:m, i * H:(i + 1) * H].unsqueeze(2).to_broadcast([m, H, XD]),
                                ALU.mult).then_inc(kn_ready, 1)
                    pool.wait_ge(x_bv_ready, 1)
                    for g in range(QUADS):
                        pool.wait_ge(o_norm_ready, g + 1)
                        cols = x_sb[:, :, g * 4 * XD:(g + 1) * 4 * XD]
                        pool.tensor_tensor(cols, cols, o_norm[:].rearrange("p t j d -> p t (j d)"),
                                           ALU.add).then_inc(x2_part, 1)

                @block.tensor
                def _(pe):
                    def turn_k(c):
                        m = rows_of(c)
                        pe.wait_ge(k_tok_ready, c + 1)
                        if c >= 2:
                            pe.wait_ge(k_aug_a, c - 1)
                            pe.wait_ge(k_aug_b, c - 1)
                        for p in range(PAIRS):
                            out = banks[:, 2 + 2 * (c % 2) + p // 4, (p % 4) * P:(p % 4) * P + m]
                            last = pe.transpose(
                                out, k_tok[c % 2][0:m, 2 * p:2 * p + 2, :].bitcast(F32)
                                .rearrange("p h d -> p (h d)"), ident[0:m, 0:m])
                        last.then_inc(kt_psum, 1)

                    def keys_values(c):
                        m, g, i = rows_of(c), c // 4, c % 4
                        if i == 0 and g >= 2:
                            pe.wait_ge(ct_lo_ready, g - 1)
                        if c >= 2:
                            pe.wait_ge(k_out, c - 1)
                            pe.wait_ge(v_ready, c - 1)
                        n = 0
                        for k in range(KD):
                            for u, w in ((ct_hi, wkv_hi), (ct_hi, wkv_lo), (ct_lo, wkv_hi)):
                                last = pe.matmul(banks[0:m, c % 2, :],
                                                 u[g % 2][:, k, i * P:i * P + m], w[:, k, :],
                                                 start=(n == 0), stop=(n == 3 * KD - 1))
                                n += 1
                        last.then_inc(kv_psum, 1)

                    def turn_x():
                        for c in range(KD):
                            for t in range(TT):
                                last = pe.transpose(banks[:, 6 + c, t * P:(t + 1) * P],
                                                    xn[:, t, c * P:(c + 1) * P], ident[:])
                            last.then_inc(xt_psum, 1)

                    def project_q():
                        pe.wait_ge(xt_ready, KD)
                        for t in range(TT):
                            for c in range(KD):
                                last = pe.matmul(banks[:, 6 + t // 2, (t % 2) * D:(t % 2 + 1) * D],
                                                 xt[:, c, t * P:(t + 1) * P],
                                                 wq_sb[:, c, :], start=(c == 0), stop=(c == KD - 1))
                            if t % 2 == 1:
                                last.then_inc(q_psum, 1)

                    def turn_q(p, done, after_a, after_b):
                        if p >= 2:
                            pe.wait_ge(after_a, p - 1)
                            pe.wait_ge(after_b, p - 1)
                        for t in range(TT):
                            last = pe.transpose(
                                banks[:, 6 + p % 2, t * P:(t + 1) * P],
                                q_tok[:, t, 2 * p:2 * p + 2, :].bitcast(F32)
                                .rearrange("p h d -> p (h d)"), ident[:])
                        last.then_inc(done, 1)

                    for step in range(KT + LAG_K):
                        if step < KT:
                            keys_values(step)
                        if step >= LAG_K:
                            turn_k(step - LAG_K)
                        if step == TURN_X_AT:
                            turn_x()
                        if step == PROJECT_Q_AT:
                            project_q()
                        if step == TURN_Q_AT:
                            pe.wait_ge(q_tok_ready, 1)
                        if TURN_Q_AT <= step < TURN_Q_AT + PAIRS:
                            turn_q(step - TURN_Q_AT, qt_psum, q_aug_a, q_aug_b)
                    pe.wait_ge(q_aug_a, PAIRS)
                    pe.wait_ge(q_aug_b, PAIRS)
                    pe.wait_ge(k_aug_a, KT)
                    pe.wait_ge(k_aug_b, KT)
                    with pe.If(pe.value_load(unsafe[0:1, 0:1], min_val=0, max_val=1) > 0):
                        for n in range(2 * H * TT):
                            h, t, half = n // (2 * TT), n // 2 % TT, n % 2
                            if n >= 2:
                                pe.wait_ge(max_ready, n - 1)
                            for i in range(2):
                                at = SPAN_AT[2 * half + i]
                                last = pe.matmul(banks[:, 2 * (n % 2) + i, 0:SPAN],
                                                 q_aug[:, h, t * P:(t + 1) * P],
                                                 k_aug[:, h // 2, at:at + SPAN], start=True, stop=True)
                            last.then_inc(max_psum, 1)
                        pe.wait_ge(shift_ready, 1)
                        for p in range(PAIRS):
                            turn_q(p, qt2_psum, q2_aug_a, q2_aug_b)
                        pe.wait_ge(q2_aug_a, PAIRS)
                        pe.wait_ge(q2_aug_b, PAIRS)
                    with pe.Else():
                        pe.nop()

                    def scores(n):
                        g, c, half, m = unit(n)
                        if n >= DEEP:
                            pe.wait_ge(probs_ready, n - DEEP + 1)
                        for i in range(2):
                            h = 4 * g + 2 * half + i
                            last = pe.matmul(banks[0:m, 2 * (n % DEEP) + i, :],
                                             k_aug[:, h // 2, c * P:c * P + m], q_aug[:, h, :],
                                             start=True, stop=True)
                        last.then_inc(s_psum, 1)

                    def times_v(n):
                        g, c, half, m = unit(n)
                        pe.wait_ge(probs_ready, n + 1)
                        if c == 0 and g >= 1:
                            pe.wait_ge(o_ready, g)
                        for j in range(4):
                            last = pe.matmul(banks[32 * j:32 * j + XD + 1, 6, :],
                                             v_one[0:m, c, 4 * g + j, :],
                                             probs[0:m, (n - 1 + j // 2) % RING, j % 2, :],
                                             start=(c == 0), stop=(c == KT - 1))
                        last.then_inc(pv_done, 1)
                        if c == KT - 1:
                            turn_o.append(g)

                    def turn_heads(g):
                        pe.wait_ge(o_ready, g + 1)
                        if g >= 1:
                            pe.wait_ge(o_norm_ready, g)
                        for t in range(TT):
                            last = pe.transpose(banks[:, 7, t * P:(t + 1) * P],
                                                o_sb[g % 2][:, t * P:(t + 1) * P], ident[:])
                        last.then_inc(ot_psum, 1)

                    turn_o = []
                    for s in range(UNITS + LAG):
                        if s < UNITS:
                            scores(s)
                        if s % (2 * KT) == LAG + 6 and turn_o:
                            turn_heads(turn_o.pop())
                        if s >= LAG and (s - LAG) % 2 == 1:
                            times_v(s - LAG)
                    turn_heads(turn_o.pop())

                @block.scalar
                def _(act):
                    def cut(g):
                        lo, hi = GROUPS[g]
                        n = min(M_KEYS, hi * P) - lo * P
                        act.wait_ge(ctx_in[g % 2], 16)
                        act.wait_ge(kv_psum, GROUPS[g - 2][1])
                        act.activation(ct_hi[g % 2][:, :, 0:n], raw[g % 2][:, :, 0:n], ACT.Copy
                                       ).then_inc(ct_hi_ready, 1)

                    def move_k(c):
                        m = rows_of(c)
                        act.wait_ge(kt_psum, c + 1)
                        act.activation(k_aug[:, 0:4, c * P:c * P + m],
                                       banks[:, 2 + 2 * (c % 2), :].rearrange("p (a k) -> p a k", a=4)
                                       [:, :, 0:m], ACT.Copy).then_inc(k_aug_a, 1)

                    def move_kv(c):
                        m = rows_of(c)
                        act.wait_ge(kv_psum, c + 1)
                        if c % 4 == 0 and c >= 8:
                            act.wait_ge(kn_ready, c - 4)
                        act.activation(kb[c // 4 % 2][0:m, c % 4, :], banks[0:m, c % 2, 0:D], ACT.Copy
                                       ).then_inc(k_out, 1)
                        act.activation(v_one[0:m, c, :, 0:XD],
                                       banks[0:m, c % 2, D:2 * D].rearrange("p (h d) -> p h d", h=H),
                                       ACT.Copy).then_inc(v_ready, 1)

                    def high_k(c):
                        m = rows_of(c)
                        act.wait_ge(kn_ready, c + 1)
                        if c >= 2:
                            act.wait_ge(kt_psum, c - 1)
                        slots = k_tok[c % 2][0:m, :, :].rearrange("p h (s d) -> p h s d", s=4)
                        act.activation(slots[:, :, 0:3:2, :],
                                       sq[c // 4 % 2][0:m, c % 4, :]
                                       .rearrange("p (h d) -> p h d", h=H).unsqueeze(2)
                                       .to_broadcast([m, H, 2, XD]), ACT.Copy
                                       ).then_inc(k_hi_ready, 1)

                    def move_x():
                        for c in range(KD):
                            act.wait_ge(xt_psum, c + 1)
                            act.activation(xt[:, c, :], banks[:, 6 + c, :], ACT.Copy
                                           ).then_inc(xt_ready, 1)

                    def high_q():
                        act.wait_ge(q_biased, TT + 1)
                        for t in range(TT):
                            last = act.activation(
                                q_tok[:, t, :, 0:2 * XD].rearrange("p h (s d) -> p h s d", s=2),
                                qb[:, t, :].rearrange("p (h d) -> p h d", h=H).unsqueeze(2)
                                .to_broadcast([P, H, 2, XD]), ACT.Copy)
                        last.then_inc(q_hi_ready, 1)

                    def evacuate_q(p, done, ready):
                        act.wait_ge(done, p + 1)
                        act.activation(q_aug[0:SLOT, 2 * p, :], banks[0:SLOT, 6 + p % 2, :], ACT.Copy
                                       ).then_inc(ready, 1)

                    for step in range(KT + LAG_K):
                        if step >= LAG_K:
                            high_k(step - LAG_K)
                        if step < KT:
                            move_kv(step)
                        if step > LAG_K:
                            move_k(step - LAG_K - 1)
                        if step == TURN_X_AT:
                            move_x()
                        if step == HIGH_Q_AT:
                            high_q()
                        if TURN_Q_AT <= step < TURN_Q_AT + PAIRS:
                            evacuate_q(step - TURN_Q_AT, qt_psum, q_aug_a)
                        if step in CUT_AFTER:
                            cut(2 + CUT_AFTER.index(step))
                    move_k(KT - 1)

                    with act.If(act.value_load(unsafe[0:1, 0:1], min_val=0, max_val=1) > 0):
                        for p in range(PAIRS):
                            evacuate_q(p, qt2_psum, q2_aug_a)
                    with act.Else():
                        act.nop()
                    for n in range(UNITS):
                        g, c, half, m = unit(n)
                        act.wait_ge(s_psum, n + 1)
                        if n >= RING:
                            act.wait_ge(pv_done, (n - RING) // 2 + 1)
                        act.activation(probs[0:m, n % RING, :, :],
                                       banks[0:m, 2 * (n % DEEP):2 * (n % DEEP) + 2, :], ACT.Exp
                                       ).then_inc(probs_ready, 1)

                @block.vector
                def _(dve):
                    chain = Chain(dve, dve_chain)
                    def cut(g):
                        lo, hi = GROUPS[g]
                        n = min(M_KEYS, hi * P) - lo * P
                        dve.wait_ge(ct_hi_ready, g - 1)
                        dve.tensor_tensor(ct_lo[g % 2][:, :, 0:n], raw[g % 2][:, :, 0:n],
                                          ct_hi[g % 2][:, :, 0:n].bitcast(F32), ALU.subtract
                                          ).then_inc(ct_lo_ready, 1)

                    def evacuate_q(p, done, ready):
                        dve.wait_ge(done, p + 1)
                        dve.tensor_copy(q_aug[SLOT:P, 2 * p + 1, :], banks[SLOT:P, 6 + p % 2, :]
                                        ).then_inc(ready, 1)

                    def rms_norm(x, tiles, m, rms, done=None):
                        n = tiles * H
                        chain.then_wait(dve.tensor_reduce(
                            square_sum[0:m, 0:n], x.rearrange("p t (h d) -> p (t h) d", h=H), AX.X, ALU.add))
                        chain.then_wait(dve.tensor_scalar(square_sum[0:m, 0:n], square_sum[0:m, 0:n],
                                                          1.0 / XD, RMS_EPS, ALU.mult, ALU.add))
                        rsqrt(dve, chain, rms[0:m, 0:n], square_sum[0:m, 0:n], rms_tmp[0:m, 0:n], done)

                    def low_k(c):
                        m = rows_of(c)
                        dve.wait_ge(k_hi_ready, c + 1)
                        dve.tensor_tensor(k_tok[c % 2][0:m, :, XD:2 * XD],
                                          sq[c // 4 % 2][0:m, c % 4, :]
                                          .rearrange("p (h d) -> p h d", h=H),
                                          k_tok[c % 2][0:m, :, 0:XD].bitcast(F32), ALU.subtract
                                          ).then_inc(k_tok_ready, 1)

                    def move_k(c):
                        m = rows_of(c)
                        dve.wait_ge(kt_psum, c + 1)
                        dve.tensor_copy(k_aug[:, 4:8, c * P:c * P + m],
                                        banks[:, 3 + 2 * (c % 2), :].rearrange("p (a k) -> p a k", a=4)
                                        [:, :, 0:m]).then_inc(k_aug_b, 1)

                    def normalise_q():
                        for n in range(2):
                            dve.wait_ge(q_psum, n + 1)
                            dve.tensor_tensor(qb[:, 2 * n:2 * n + 2, :],
                                              banks[:, 6 + n, :].rearrange("p (t d) -> p t d", t=2),
                                              bq_row[:].unsqueeze(1).to_broadcast([P, 2, D]), ALU.add
                                              ).then_inc(q_biased, TT // 2)
                        dve.wait_ge(q_biased, TT)
                        chain.then_wait(dve.tensor_tensor(xn[:], qb[:], qb[:], ALU.mult))
                        rms_norm(xn[:], TT, P, rms_q)
                        heads = qb[:].rearrange("p t (h d) -> p (t h) d", h=H)
                        chain.then_wait(dve.tensor_tensor(
                            heads, heads, rms_q[:].unsqueeze(2).to_broadcast([P, TT * H, XD]), ALU.mult))
                        dve.tensor_tensor(heads, heads, gain[:].unsqueeze(1)
                                          .to_broadcast([P, TT * H, XD]), ALU.mult
                                          ).then_inc(q_biased, 1)

                    def low_q():
                        dve.memset(q_tok[:, :, :, SHIFT:SHIFT + 1].bitcast(F32), 0.0)
                        dve.wait_ge(q_hi_ready, 1)
                        for t in range(TT):
                            last = dve.tensor_tensor(q_tok[:, t, :, 2 * XD:3 * XD],
                                                     qb[:, t, :].rearrange("p (h d) -> p h d", h=H),
                                                     q_tok[:, t, :, 0:XD].bitcast(F32), ALU.subtract)
                        last.then_inc(q_tok_ready, 1)

                    for step in range(KT + LAG_K):
                        if step >= LAG_K:
                            low_k(step - LAG_K)
                        if step > LAG_K:
                            move_k(step - LAG_K - 1)
                        if step < KT and step in ENDS:
                            g = ENDS.index(step)
                            lo, hi = GROUPS[g]
                            dve.wait_ge(sq_ready, hi)
                            if g >= 1:
                                dve.wait_ge(kn_ready, lo)
                            rms_norm(sq[g % 2][0:rows_of(lo), 0:hi - lo, :], hi - lo, rows_of(lo),
                                     rms, rms_ready)
                        if step == NORM_Q_AT:
                            normalise_q()
                        if step == LOW_Q_AT:
                            low_q()
                        if TURN_Q_AT <= step < TURN_Q_AT + PAIRS:
                            evacuate_q(step - TURN_Q_AT, qt_psum, q_aug_b)
                        if step in CUT_AFTER:
                            cut(2 + CUT_AFTER.index(step))
                    move_k(KT - 1)

                    with dve.If(dve.value_load(unsafe[0:1, 0:1], min_val=0, max_val=1) > 0):
                        for n in range(2 * H * TT):
                            h, t, half = n // (2 * TT), n // 2 % TT, n % 2
                            dve.wait_ge(max_psum, n + 1)
                            last = dve.tensor_reduce(maxima[:, h, t, half:half + 1],
                                                     banks[:, 2 * (n % 2):2 * (n % 2) + 2, 0:SPAN],
                                                     AX.XY, ALU.max)
                            last.then_inc(max_ready, 1)
                        dve.wait_ge(max_ready, 2 * H * TT)
                        for t in range(TT):
                            last = dve.tensor_reduce(q_tok[:, t, :, SHIFT:SHIFT + 1], maxima[:, :, t, :],
                                                     AX.X, ALU.max, negate=True)
                        last.then_inc(shift_ready, 1)
                        for p in range(PAIRS):
                            evacuate_q(p, qt2_psum, q2_aug_b)
                    with dve.Else():
                        dve.nop()
                    dve.wait_ge(kv_psum, KT)
                    for g in range(2):
                        dve.wait_ge(next_in[g], 16)
                        dve.tensor_copy(ct_hi[g][:], raw[g][:]).then_inc(next_hi, 1)
                        dve.wait_ge(next_hi, g + 1)
                        dve.tensor_tensor(ct_lo[g][:], raw[g][:], ct_hi[g][:].bitcast(F32), ALU.subtract)
                    dve.wait_ge(x_next_in, 16)
                    layernorm(dve, chain, xn, xn, TT, stats, mean_var, var[:], rstd[:], tmp[:])
                    for g in range(QUADS):
                        dve.wait_ge(pv_done, KT * (g + 1))
                        dve.tensor_copy(o_sb[g % 2][:], banks[:, 6, :]).then_inc(o_ready, 1)
                        dve.wait_ge(ot_psum, g + 1)
                        heads = banks[:, 7, :].rearrange("p (t j d) -> p t j d", t=TT, j=4)
                        chain.then_wait(dve.reciprocal(rec[:], heads[:, :, :, XD:XD + 1]
                                                       .rearrange("p t j d -> p t (j d)")))
                        if g >= 1:
                            dve.wait_ge(x2_part, g)
                        dve.tensor_tensor(o_norm[:], heads[:, :, :, 0:XD],
                                          rec[:].unsqueeze(3).to_broadcast([P, TT, 4, XD]), ALU.mult
                                          ).then_inc(o_norm_ready, 1)
            nc.all_engine_barrier(sems_to_clear=range(sems[first].num, sems[-1].num + 1))
        with nc.Block() as block:
            @block.sync
            def _(sp):
                sp.wait_ge(x2_out, 16 * B + 16)
        nc.all_engine_barrier(sems_to_clear=range(sems[0].num, sems[once - 1].num + 1))


def experts(nc, x2, cls_t, score_bias, gate_up_t, down_t, out):
    CHUNKS = B * T // 512
    PER_TURN = 2 * CHUNKS
    TURNS = E_ROUTED // 2
    SENTINELS = 2
    HUGE = 3.0e38

    with ExitStack() as ctx:
        def sb(name, shape, dt=F32):
            return ctx.enter_context(nc.sbuf_tensor("mo_" + name, shape, dt))

        sems = []

        def sem(name):
            sems.append(ctx.enter_context(nc.semaphore("mo_" + name)))
            return sems[-1]

        ident = sb("ident", [P, P])
        acc = sb("acc", [P, TILES, D])
        xn = sb("xn", [P, TILES, D])
        xt_hi = sb("xt_hi", [P, KD, B * T], F32R)
        xt_lo = sb("xt_lo", [P, KD, B * T], F32R)
        cls = sb("cls", [P, KD, E_ALL])
        cls_hi = sb("cls_hi", [P, KD, E_ALL], F32R)
        cls_lo = sb("cls_lo", [P, KD, E_ALL], F32R)
        bias_row = sb("bias_row", [P, E_ALL])
        stats = sb("stats", [P, TILES, 6])
        mean_var = sb("mean_var", [P, TILES, 2])
        var = sb("var", [P, TILES])
        rstd = sb("rstd", [P, TILES])
        tmp = sb("tmp", [P, TILES])
        scores = sb("scores", [P, TILES, E_ALL])
        choice = sb("choice", [P, TILES, E_ALL + SENTINELS])
        left = sb("left", [P, TILES, E_ALL + SENTINELS])
        top = sb("top", [P, TILES, 8])
        weights = sb("weights", [P, E_ALL, TILES])
        current = [sb(f"current{i}", [P, TILES]) for i in range(2)]
        zero_w = sb("zero_w", [P, TILES])
        gu_raw = [sb(f"gu_raw{i}", [P, KD, 2 * INTER]) for i in range(2)]
        dn_raw = [sb(f"dn_raw{i}", [P, D]) for i in range(2)]
        gu_hi = [sb(f"gu_hi{i}", [P, KD, 2 * INTER], F32R) for i in range(2)]
        gu_lo = [sb(f"gu_lo{i}", [P, KD, 2 * INTER], F32R) for i in range(2)]
        dn_hi = [sb(f"dn_hi{i}", [P, D], F32R) for i in range(2)]
        dn_lo = [sb(f"dn_lo{i}", [P, D], F32R) for i in range(2)]
        silu = [sb(f"silu{i}", [P, 512]) for i in range(2)]
        hidden = [sb(f"hidden{i}", [P, 512]) for i in range(2)]
        h_hi = [sb(f"h_hi{i}", [P, 512], F32R) for i in range(2)]
        h_lo = [sb(f"h_lo{i}", [P, 512], F32R) for i in range(2)]
        banks = ctx.enter_context(nc.psum_tensor("mo_banks", [P, 8, 512], F32))

        logits_t = silu + hidden

        x_in = sem("x_in")
        router_in = sem("router_in")
        zeroed = sem("zeroed")
        ident_ready = sem("ident_ready")
        cls_ready = sem("cls_ready")
        xn_ready = sem("xn_ready")
        xt_psum = sem("xt_psum")
        xt_hi_ready = sem("xt_hi_ready")
        xt_lo_ready = sem("xt_lo_ready")
        lt_psum = sem("lt_psum")
        lt_out = sem("lt_out")
        logits_psum = sem("logits_psum")
        shifted = sem("shifted")
        exp_ready = sem("exp_ready")
        dve_chain = sem("dve_chain")
        gu_in = [sem("gu_in0"), sem("gu_in1")]
        w_hi_ready = sem("w_hi_ready")
        w_ready = sem("w_ready")
        gu_psum = sem("gu_psum")
        silu_ready = sem("silu_ready")
        h_ready = sem("h_ready")
        h_hi_ready = sem("h_hi_ready")
        h_lo_ready = sem("h_lo_ready")
        y_psum = sem("y_psum")
        y_added = sem("y_added")
        current_ready = sem("current_ready")
        out_done = sem("out_done")

        with nc.Block() as block:
            @block.sync
            def _(sp):
                sp.dma_start(cls[:], cls_t.rearrange("(c p) e -> p c e", p=P)).then_inc(router_in, 16)
                sp.dma_start(bias_row[:], score_bias.partition_broadcast(P)).then_inc(router_in, 16)
                x2_v = x2.rearrange("b (t p) d -> p (b t) d", p=P)
                for g in range(B):
                    sp.dma_start(acc[:, TT * g:TT * g + TT, :], x2_v[:, TT * g:TT * g + TT, :]
                                 ).then_inc(x_in, 16)

                def load(e, i):
                    sp.dma_start(gu_raw[i][:], gate_up_t[e].rearrange("(c p) n -> p c n", p=P)
                                 ).then_inc(gu_in[i], 16)
                    sp.dma_start(dn_raw[i][:], down_t[e]).then_inc(gu_in[i], 16)

                for i in range(2):
                    load(i, i)
                with sp.Fori(0, TURNS - 1) as turn:
                    for i in range(2):
                        sp.wait_ge(w_ready, turn * 2 + (i + 1))
                        load(turn * 2 + (i + 2), i)
                sp.wait_ge(y_added, 2 + TURNS * PER_TURN)
                out_v = out.rearrange("b (t p) d -> p (b t) d", p=P)
                for g in range(B):
                    sp.dma_start(out_v[:, TT * g:TT * g + TT, :], acc[:, TT * g:TT * g + TT, :]
                                 ).then_inc(out_done, 16)
                sp.wait_ge(out_done, 16 * B)

            @block.gpsimd
            def _(pool):
                pool.memset(ident[:], 0.0).then_inc(zeroed, 1)
                pool.wait_ge(zeroed, 1)
                pool.affine_select(out=ident[:], in_=ident[:], compare_op=ALU.not_equal, fill=1.0,
                                   base=0, pattern=[[-1, P]], channel_multiplier=1
                                   ).then_inc(ident_ready, 1)

                def low(done, i):
                    pool.wait_ge(w_hi_ready, done + 1)
                    pool.tensor_tensor(gu_lo[i][:], gu_raw[i][:], gu_hi[i][:].bitcast(F32), ALU.subtract)
                    pool.tensor_tensor(dn_lo[i][:], dn_raw[i][:], dn_hi[i][:].bitcast(F32), ALU.subtract
                                       ).then_inc(w_ready, 1)

                low(0, 0)
                with pool.Fori(0, TURNS - 1) as turn:
                    low(turn * 2 + 1, 1)
                    low(turn * 2 + 2, 0)
                low(E_ROUTED - 1, 1)

            @block.tensor
            def _(pe):
                pe.wait_ge(ident_ready, 1)
                for n in range(KD * B):
                    c, g = n % KD, n // KD
                    pe.wait_ge(xn_ready, g + 1)
                    for t in range(TT):
                        last = pe.transpose(banks[:, n, t * P:(t + 1) * P],
                                            xn[:, TT * g + t, c * P:(c + 1) * P], ident[:])
                    last.then_inc(xt_psum, 1)
                pe.wait_ge(cls_ready, 2)
                for g in range(B):
                    pe.wait_ge(xt_lo_ready, KD * (g + 1))
                    n = 0
                    for c in range(KD):
                        for u in (xt_hi, xt_lo):
                            for w in (cls_hi, cls_lo):
                                last = pe.matmul(banks[0:E_ALL, g, :], w[:, c, :],
                                                 u[:, c, g * T:(g + 1) * T], start=(n == 0),
                                                 stop=(n == 4 * KD - 1))
                                n += 1
                    last.then_inc(lt_psum, 1)
                for t in range(TILES):
                    g = t // TT
                    if t % TT == 0:
                        pe.wait_ge(lt_out, g + 1)
                    last = pe.transpose(banks[:, 6 + t // 8, (t % 8) * E_ALL:(t % 8 + 1) * E_ALL],
                                        logits_t[g][0:E_ALL, (t % TT) * P:(t % TT + 1) * P],
                                        ident[0:E_ALL, 0:E_ALL])
                last.then_inc(logits_psum, 1)

                def front(turn, j):
                    i, chunk = j // CHUNKS % 2, j % CHUNKS
                    if chunk == 0:
                        pe.wait_ge(w_ready, turn * 2 + (j // CHUNKS + 1))
                    if j > 0:
                        pe.wait_ge(h_ready, turn * PER_TURN + j)
                    tok = slice(chunk * 512, (chunk + 1) * 512)
                    for half in range(2):
                        cols = slice(half * INTER, (half + 1) * INTER)
                        n = 0
                        for c in range(KD):
                            for w, u in ((gu_hi, xt_hi), (gu_hi, xt_lo), (gu_lo, xt_hi)):
                                last = pe.matmul(banks[:, 2 * (j % 2) + half, :], w[i][:, c, cols],
                                                 u[:, c, tok], start=(n == 0), stop=(n == 3 * KD - 1))
                                n += 1
                    last.then_inc(gu_psum, 1)

                def back(turn, j):
                    i = j // CHUNKS
                    pe.wait_ge(h_lo_ready, turn * PER_TURN + (j + 1))
                    pe.wait_ge(y_added, turn * PER_TURN + (j + 1))
                    for t in range(4):
                        at = (t % 2) * D
                        for n, (u, w) in enumerate(((h_hi, dn_hi), (h_hi, dn_lo), (h_lo, dn_hi))):
                            last = pe.matmul(banks[:, 4 + 2 * (j % 2) + t // 2, at:at + D],
                                             u[j % 2][:, t * P:(t + 1) * P], w[i][:],
                                             start=(n == 0), stop=(n == 2))
                    last.then_inc(y_psum, 1)

                front(0, 0)
                with pe.Fori(0, TURNS - 1) as turn:
                    for j in range(PER_TURN):
                        front(turn, j + 1)
                        back(turn, j)
                for j in range(PER_TURN):
                    if j + 1 < PER_TURN:
                        front(TURNS - 1, j + 1)
                    back(TURNS - 1, j)

            @block.scalar
            def _(act):
                act.wait_ge(router_in, 32)
                act.activation(cls_hi[:], cls[:], ACT.Copy).then_inc(cls_ready, 1)
                for n in range(KD * B):
                    c, g = n % KD, n // KD
                    act.wait_ge(xt_psum, n + 1)
                    act.activation(xt_hi[:, c, g * T:(g + 1) * T], banks[:, n, :], ACT.Copy
                                   ).then_inc(xt_hi_ready, 1)
                for g in range(B):
                    act.wait_ge(lt_psum, g + 1)
                    act.activation(logits_t[g][0:E_ALL, :], banks[0:E_ALL, g, :], ACT.Copy
                                   ).then_inc(lt_out, 1)
                act.wait_ge(shifted, 1)
                act.activation(scores[:], scores[:], ACT.Exp).then_inc(exp_ready, 1)

                def front(turn, j):
                    act.wait_ge(gu_psum, turn * PER_TURN + (j + 1))
                    act.activation(silu[j % 2][:], banks[:, 2 * (j % 2), :], ACT.Silu
                                   ).then_inc(silu_ready, 1)
                    act.wait_ge(h_ready, turn * PER_TURN + (j + 2))
                    act.activation(h_hi[j % 2][:], hidden[j % 2][:], ACT.Copy).then_inc(h_hi_ready, 1)

                def cut(turn, i):
                    act.wait_ge(gu_in[i], turn * 32 + 32)
                    act.activation(gu_hi[i][:], gu_raw[i][:], ACT.Copy)
                    act.activation(dn_hi[i][:], dn_raw[i][:], ACT.Copy).then_inc(w_hi_ready, 1)

                def step(turn, j, last=False):
                    if not (last and j == PER_TURN - 1):
                        front(turn, j + 1)
                    if j == 1:
                        act.wait_ge(y_psum, turn * PER_TURN + 1)
                        cut(turn, 1)
                    if j == CHUNKS + 1 and not last:
                        act.wait_ge(y_psum, turn * PER_TURN + CHUNKS)
                        cut(turn + 1, 0)

                cut(0, 0)
                front(0, 0)
                with act.Fori(0, TURNS - 1) as turn:
                    for j in range(PER_TURN):
                        step(turn, j)
                for j in range(PER_TURN):
                    step(TURNS - 1, j, last=True)

            @block.vector
            def _(dve):
                chain = Chain(dve, dve_chain)
                dve.memset(choice[:, :, E_ALL:], HUGE).then_inc(h_ready, 1)
                dve.wait_ge(cls_ready, 1)
                dve.tensor_tensor(cls_lo[:], cls[:], cls_hi[:].bitcast(F32), ALU.subtract
                                  ).then_inc(cls_ready, 1)
                dve.wait_ge(x_in, 16 * B)
                layernorm(dve, chain, xn, acc, TILES, stats, mean_var, var[:], rstd[:], tmp[:],
                          done=xn_ready)
                for n in range(KD * B):
                    c, g = n % KD, n // KD
                    dve.wait_ge(xt_hi_ready, n + 1)
                    dve.tensor_tensor(xt_lo[:, c, g * T:(g + 1) * T], banks[:, n, :],
                                      xt_hi[:, c, g * T:(g + 1) * T].bitcast(F32), ALU.subtract
                                      ).then_inc(xt_lo_ready, 1)
                dve.wait_ge(logits_psum, 1)
                logits = banks[:, 6:8, 0:8 * E_ALL].rearrange("p b (t e) -> p b t e", e=E_ALL)
                grouped = scores[:].rearrange("p (b t) e -> p b t e", b=2)
                for half in range(2):
                    last = dve.tensor_reduce(tmp[:, 8 * half:8 * half + 8], logits[:, half], AX.X, ALU.max)
                chain.then_wait(last)
                for half in range(2):
                    last = dve.tensor_tensor(grouped[:, half], logits[:, half],
                                             tmp[:, 8 * half:8 * half + 8].unsqueeze(2)
                                             .to_broadcast([P, 8, E_ALL]), ALU.subtract)
                last.then_inc(shifted, 1)
                dve.wait_ge(exp_ready, 1)
                chain.then_wait(dve.tensor_reduce(var[:], scores[:], AX.X, ALU.add))
                chain.then_wait(dve.reciprocal(rstd[:], var[:]))
                chain.then_wait(dve.tensor_tensor(scores[:], scores[:],
                                                  rstd[:].unsqueeze(2).to_broadcast([P, TILES, E_ALL]),
                                                  ALU.mult))
                chain.then_wait(dve.tensor_tensor(choice[:, :, 0:E_ALL], scores[:],
                                                  bias_row[:].unsqueeze(1)
                                                  .to_broadcast([P, TILES, E_ALL]), ALU.add))
                for t in range(TILES):
                    last = dve.max(top[:, t, :], choice[:, t, :])
                chain.then_wait(last)
                for t in range(TILES):
                    last = dve.match_replace(left[:, t, :], top[:, t, :], choice[:, t, :], -HUGE)
                chain.then_wait(last)
                chain.then_wait(dve.tensor_tensor(left[:, :, 0:E_ALL], left[:, :, 0:E_ALL],
                                                  choice[:, :, 0:E_ALL], ALU.not_equal))
                chain.then_wait(dve.scalar_tensor_tensor(
                    out=weights[:].rearrange("p e t -> p t e"), in0=left[:, :, 0:E_ALL],
                    scalar=ROUTE_SCALE, in1=scores[:], op0=ALU.mult, op1=ALU.mult))
                chain.then_wait(dve.tensor_reduce(
                    zero_w[:], weights[:, E_ROUTED:, :].rearrange("p e t -> p t e"), AX.X, ALU.add))
                for t in range(TILES):
                    last = dve.scalar_tensor_tensor(out=acc[:, t, :], in0=xn[:, t, :],
                                                    scalar=zero_w[:, t:t + 1], in1=acc[:, t, :],
                                                    op0=ALU.mult, op1=ALU.add)
                last.then_inc(y_added, 2)

                def front(turn, j):
                    if j % CHUNKS == 0:
                        i = j // CHUNKS % 2
                        dve.tensor_copy(current[i][:], weights[:, turn * 2 + j // CHUNKS, :]
                                        ).then_inc(current_ready, 1)
                    dve.wait_ge(silu_ready, turn * PER_TURN + (j + 1))
                    dve.tensor_tensor(hidden[j % 2][:], banks[:, 2 * (j % 2) + 1, :], silu[j % 2][:],
                                      ALU.mult).then_inc(h_ready, 1)
                    dve.wait_ge(h_hi_ready, turn * PER_TURN + (j + 1))
                    dve.tensor_tensor(h_lo[j % 2][:], hidden[j % 2][:], h_hi[j % 2][:].bitcast(F32),
                                      ALU.subtract).then_inc(h_lo_ready, 1)

                def back(turn, j):
                    i, chunk = j // CHUNKS, j % CHUNKS
                    dve.wait_ge(current_ready, turn * 2 + (i + 1))
                    dve.wait_ge(y_added, turn * PER_TURN + (j + 2))
                    dve.wait_ge(y_psum, turn * PER_TURN + (j + 1))
                    for t in range(4):
                        tile = chunk * 4 + t
                        last = dve.scalar_tensor_tensor(
                            out=acc[:, tile, :], in0=banks[:, 4 + 2 * (j % 2) + t // 2,
                                                           (t % 2) * D:(t % 2 + 1) * D],
                            scalar=current[i][:, tile:tile + 1], in1=acc[:, tile, :],
                            op0=ALU.mult, op1=ALU.add)
                    last.then_inc(y_added, 1)

                front(0, 0)
                with dve.Fori(0, TURNS - 1) as turn:
                    for j in range(PER_TURN):
                        front(turn, j + 1)
                        back(turn, j)
                for j in range(PER_TURN):
                    if j + 1 < PER_TURN:
                        front(TURNS - 1, j + 1)
                    back(TURNS - 1, j)


def decoder_layer(nc, x, ctx_t, wq, wk, wv, wo, bo, bias_rev, xwq_t, xbq, xwkv_t, xbkv, q_gamma,
                  k_gamma, cls_t, score_bias, gate_up_t, down_t, out):
    ext_scratch = nc.dram_tensor("extended_bias", (H, T + P), F32).ap()
    x1 = nc.dram_tensor("x1", (B, T, D), F32).ap()
    x2 = nc.dram_tensor("x2", (B, T, D), F32).ap()
    self_attention(nc, x, wq, wk, wv, wo, bo, bias_rev, ext_scratch, x1)
    cross_attention(nc, x1, ctx_t, xwq_t, xbq, xwkv_t, xbkv, q_gamma, k_gamma, x2)
    experts(nc, x2, cls_t, score_bias, gate_up_t, down_t, out)


def kernel(**inputs):
    import numpy as np
    import concourse.bacc as bacc
    from concourse.bass_utils import run_bass_kernel_spmd

    given = {k: np.asarray(v) for k, v in inputs.items()}
    wkv = given["L0_xattn_Wkv"].reshape(D, 2, D).transpose(2, 1, 0).reshape(D, 2 * D)
    bkv = given["L0_xattn_bkv"].reshape(D, 2).transpose(1, 0).reshape(2 * D)
    arrays = {
        "x": given["x"],
        "ctx_t": given["ctx_1024"].transpose(0, 2, 1),
        "wq": given["L0_attn_Wq"],
        "wk": given["L0_attn_Wk"],
        "wv": given["L0_attn_Wv"],
        "wo": given["L0_attn_Wo"],
        "bo": given["L0_attn_bo"],
        "bias_rev": given["L0_attn_rel_pos_bias"][:, ::-1],
        "xwq_t": given["L0_xattn_Wq"].transpose(1, 0),
        "xbq": given["L0_xattn_bq"],
        "xwkv_t": wkv,
        "xbkv": bkv,
        "q_gamma": given["L0_xattn_q_gamma"],
        "k_gamma": given["L0_xattn_k_gamma"],
        "cls_t": given["L0_ffn_classifier_weight"].transpose(1, 0),
        "score_bias": given["L0_ffn_e_score_correction_bias"],
        "gate_up_t": given["L0_ffn_gate_up_proj"].transpose(0, 2, 1),
        "down_t": given["L0_ffn_down_proj"].transpose(0, 2, 1),
    }
    arrays = {f"in_{k}": np.ascontiguousarray(v) for k, v in arrays.items()}
    nc = bacc.Bacc("TRN2", target_bir_lowering=False, num_devices=1)
    args = [nc.dram_tensor(k, v.shape, mybir.dt.from_np(v.dtype), kind="ExternalInput").ap()
            for k, v in arrays.items()]
    out = nc.dram_tensor("out", (B, T, D), F32, kind="ExternalOutput").ap()
    decoder_layer(nc, *args, out)
    r = run_bass_kernel_spmd(nc, [arrays], core_ids=[0])
    return r.results[0]["out"]
```
